# Optimizing a Trainium2 kernel written in Bass

```python
import numpy as np
import jax
import jax.numpy as jnp

def _softmax(x, axis=-1):
    return jax.nn.softmax(x, axis=axis)

def _gelu(x):
    return jax.nn.gelu(x, approximate=True)

def _silu(x):
    return jax.nn.silu(x)

def _sigmoid(x):
    return jax.nn.sigmoid(x)

def _layernorm(x, axis=-1, eps=1e-05):
    m = jnp.mean(x, axis=axis, keepdims=True)
    v = jnp.var(x, axis=axis, keepdims=True)
    return (x - m) / jnp.sqrt(v + eps)

def _scatter_add(tgt, idx, src, axis=0):
    return tgt.at[idx].add(src)

def _segment_sum(src, seg, n):
    return jax.ops.segment_sum(src, seg, n)
kernel_name = 'mk_seq_postln_d1_jaxref_r8_422bff'

def setup_inputs(seed: int=0):
    np.random.seed(seed)
    _w = jnp.asarray

    def _L0_attn_setup():
        import jax, jax.numpy as jnp
        import numpy as np
        B, T, C, R = (8, 128, 128, 64)
        EPS = 1e-05
        key = jax.random.key(seed)
        ks = jax.random.split(key, 8)
        x = jax.random.normal(ks[0], (B, T, C), dtype=jnp.float32)
        W_attn = jax.random.normal(ks[1], (3 * C, C), dtype=jnp.float32) * 0.02
        W_proj = jax.random.normal(ks[2], (C, C), dtype=jnp.float32) * 0.02
        lora_attn_A = jax.random.normal(ks[3], (C, R), dtype=jnp.float32) * 0.02
        lora_attn_B = jax.random.normal(ks[4], (R, 3 * C), dtype=jnp.float32) * 0.02
        lora_proj_A = jax.random.normal(ks[5], (C, R), dtype=jnp.float32) * 0.02
        lora_proj_B = jax.random.normal(ks[6], (R, C), dtype=jnp.float32) * 0.02
        bn_gamma = jnp.ones((3 * C,), dtype=jnp.float32)
        bn_beta = jnp.zeros((3 * C,), dtype=jnp.float32)
        return {'x': x, 'W_attn': W_attn, 'W_proj': W_proj, 'lora_attn_A': lora_attn_A, 'lora_attn_B': lora_attn_B, 'lora_proj_A': lora_proj_A, 'lora_proj_B': lora_proj_B, 'bn_gamma': bn_gamma, 'bn_beta': bn_beta}
    _L0_attn_in = _L0_attn_setup()

    def _L0_ffn_setup():
        import jax, jax.numpy as jnp
        import numpy as np
        B, L, D = (4, 256, 128)
        E, K, S = (8, 2, 2)
        F = 176
        SCALE = 1.0
        INIT = 0.02

        def _swiglu(x, wg, wu, wd):
            return jax.nn.silu(x @ wg) * (x @ wu) @ wd
        key = jax.random.key(seed)
        ks = jax.random.split(key, 8)
        return {'hidden_states': jax.random.normal(ks[0], (B, L, D), jnp.float32), 'gate_w': jax.random.normal(ks[1], (D, E), jnp.float32) * INIT, 'exp_gate': jax.random.normal(ks[2], (E, D, F), jnp.float32) * INIT, 'exp_up': jax.random.normal(ks[3], (E, D, F), jnp.float32) * INIT, 'exp_down': jax.random.normal(ks[4], (E, F, D), jnp.float32) * INIT, 'sh_gate': jax.random.normal(ks[5], (S, D, F), jnp.float32) * INIT, 'sh_up': jax.random.normal(ks[6], (S, D, F), jnp.float32) * INIT, 'sh_down': jax.random.normal(ks[7], (S, F, D), jnp.float32) * INIT}
    _L0_ffn_in = _L0_ffn_setup()
    _d = {'L0_attn_x': _L0_attn_in['x'], 'L0_attn_W_attn': _L0_attn_in['W_attn'], 'L0_attn_W_proj': _L0_attn_in['W_proj'], 'L0_attn_lora_attn_A': _L0_attn_in['lora_attn_A'], 'L0_attn_lora_attn_B': _L0_attn_in['lora_attn_B'], 'L0_attn_lora_proj_A': _L0_attn_in['lora_proj_A'], 'L0_attn_lora_proj_B': _L0_attn_in['lora_proj_B'], 'L0_attn_bn_gamma': _L0_attn_in['bn_gamma'], 'L0_attn_bn_beta': _L0_attn_in['bn_beta'], 'L0_ffn_gate_w': _L0_ffn_in['gate_w'], 'L0_ffn_exp_gate': _L0_ffn_in['exp_gate'], 'L0_ffn_exp_up': _L0_ffn_in['exp_up'], 'L0_ffn_exp_down': _L0_ffn_in['exp_down'], 'L0_ffn_sh_gate': _L0_ffn_in['sh_gate'], 'L0_ffn_sh_up': _L0_ffn_in['sh_up'], 'L0_ffn_sh_down': _L0_ffn_in['sh_down']}
    _x0 = _d['L0_attn_x']
    _d['L0_attn_x'] = jax.random.normal(jax.random.fold_in(jax.random.key(seed), 1), (4, 512, 128), dtype=_x0.dtype)
    del _x0
    return _d

def reference(L0_attn_x, L0_attn_W_attn, L0_attn_W_proj, L0_attn_lora_attn_A, L0_attn_lora_attn_B, L0_attn_lora_proj_A, L0_attn_lora_proj_B, L0_attn_bn_gamma, L0_attn_bn_beta, L0_ffn_gate_w, L0_ffn_exp_gate, L0_ffn_exp_up, L0_ffn_exp_down, L0_ffn_sh_gate, L0_ffn_sh_up, L0_ffn_sh_down):

    def _L0_attn_ref(x, W_attn, W_proj, lora_attn_A, lora_attn_B, lora_proj_A, lora_proj_B, bn_gamma, bn_beta):
        import jax, jax.numpy as jnp
        import numpy as np
        B, T, C, R = (8, 128, 128, 64)
        EPS = 1e-05
        Bb, Tt, Cc = x.shape
        Wm_attn = W_attn + (lora_attn_A @ lora_attn_B).reshape(W_attn.shape)
        xa = jnp.einsum('btc,dc->btd', x, Wm_attn)
        mean = xa.mean(axis=(0, 1))
        var = xa.var(axis=(0, 1))
        xa = (xa - mean) * jax.lax.rsqrt(var + EPS) * bn_gamma + bn_beta
        q, k, v = jnp.split(xa, 3, axis=-1)
        scale = 1.0 / jnp.sqrt(jnp.asarray(Cc, dtype=x.dtype))
        att = jnp.einsum('btc,bsc->bts', q, k) * scale
        causal = jnp.tril(jnp.ones((Tt, Tt), dtype=bool))
        att = jnp.where(causal[None, :, :], att, -jnp.inf)
        att = jax.nn.softmax(att, axis=-1)
        y = jnp.einsum('bts,bsc->btc', att, v)
        y = jnp.einsum('btc,dc->btd', y, W_proj)
        Wm_proj = W_proj + (lora_proj_A @ lora_proj_B).reshape(W_proj.shape)
        y = jnp.einsum('btc,dc->btd', y, Wm_proj)
        return y

    def _L0_ffn_ref(hidden_states, gate_w, exp_gate, exp_up, exp_down, sh_gate, sh_up, sh_down):
        import jax, jax.numpy as jnp
        import numpy as np
        B, L, D = (4, 256, 128)
        E, K, S = (8, 2, 2)
        F = 176
        SCALE = 1.0
        INIT = 0.02

        def _swiglu(x, wg, wu, wd):
            return jax.nn.silu(x @ wg) * (x @ wu) @ wd
        Bx, Lx, Dx = hidden_states.shape
        x = hidden_states.reshape(-1, Dx)
        T = x.shape[0]
        shared = jnp.zeros_like(x)
        for i in range(sh_gate.shape[0]):
            shared = shared + _swiglu(x, sh_gate[i], sh_up[i], sh_down[i])
        logits = x @ gate_w
        probs = jax.nn.softmax(logits.astype(jnp.float32), axis=-1)
        w, sel = jax.lax.top_k(probs, K)
        w = w / jnp.sum(w, axis=-1, keepdims=True)
        w = w.astype(hidden_states.dtype)
        Wte = jnp.zeros((T, exp_gate.shape[0]), hidden_states.dtype)
        Wte = Wte.at[jnp.arange(T)[:, None], sel].add(w)
        routed = jnp.zeros_like(x)
        for e in range(exp_gate.shape[0]):
            routed = routed + Wte[:, e:e + 1] * _swiglu(x, exp_gate[e], exp_up[e], exp_down[e])
        out = shared + SCALE * routed
        return out.reshape(Bx, Lx, Dx)
    x = L0_attn_x
    x = _layernorm(x + _L0_attn_ref(x, L0_attn_W_attn, L0_attn_W_proj, L0_attn_lora_attn_A, L0_attn_lora_attn_B, L0_attn_lora_proj_A, L0_attn_lora_proj_B, L0_attn_bn_gamma, L0_attn_bn_beta), axis=-1)
    x = _layernorm(x + _L0_ffn_ref(x, L0_ffn_gate_w, L0_ffn_exp_gate, L0_ffn_exp_up, L0_ffn_exp_down, L0_ffn_sh_gate, L0_ffn_sh_up, L0_ffn_sh_down), axis=-1)
    return x

_drawn_inputs = setup_inputs


def setup_inputs(seed=0):
    import zlib

    import numpy as np

    out = dict(_drawn_inputs(seed))
    spreads = {'L0_attn_bn_gamma': (1.0, 0.6), 'L0_attn_bn_beta': (0.0, 0.8)}
    factors = {'L0_attn_W_attn': 5.357,
     'L0_attn_W_proj': 4.666,
     'L0_attn_lora_attn_A': 8.0,
     'L0_attn_lora_attn_B': 8.0,
     'L0_attn_lora_proj_A': 8.0,
     'L0_attn_lora_proj_B': 8.0,
     'L0_ffn_gate_w': 8.0,
     'L0_ffn_exp_gate': 8.0,
     'L0_ffn_exp_up': 8.0,
     'L0_ffn_exp_down': 8.0,
     'L0_ffn_sh_gate': 5.932,
     'L0_ffn_sh_up': 5.907,
     'L0_ffn_sh_down': 5.878}
    for name, (base, spread) in spreads.items():
        noise = np.random.default_rng([zlib.crc32(name.encode()), seed]).standard_normal(out[name].shape)
        drawn = base * np.exp(spread * noise) if base else spread * noise
        out[name] = jnp.asarray(drawn.astype(out[name].dtype))
    for name, factor in factors.items():
        out[name] = (out[name] * factor).astype(out[name].dtype)
    return out
```

```python
from contextlib import ExitStack

import numpy as np

import concourse.bass as bass
from concourse import mybir

ALU = mybir.AluOpType
ACT = mybir.ActivationFunctionType
AX = mybir.AxisListType
F32 = mybir.dt.float32
F32R = mybir.dt.float32r

P = 128
EPS = 1e-5
MASKED = -1.0e30
BIG = 3.0e38
LO_ROW = 32


def need(eng, sem, value):
    if isinstance(value, int) and value <= 0:
        return
    eng.wait_ge(sem, value)


class Steps:

    def __init__(self, eng, sem, base=0):
        self.eng, self.sem, self.base, self.n = eng, sem, base, 0

    def done(self, ins):
        self.n += 1
        ins.then_inc(self.sem, 1)

    def wait(self):
        self.eng.wait_ge(self.sem, self.base + self.n)


def block_kernel(nc, x, W_attn, W_proj, attn_A, attn_B, proj_A, proj_B, bn_gamma, bn_beta,
                 gate_w, exp_gate, exp_up, exp_down, sh_gate, sh_up, sh_down, out):
    NB, SEQ, C = x.shape
    R = attn_A.shape[1]
    D3 = W_attn.shape[0]
    NJ = D3 // C
    E, _, F = exp_gate.shape
    S = sh_gate.shape[0]
    NT = SEQ // P
    NTOK = NB * SEQ
    SCALE = float(C) ** -0.5
    SHF = S * F
    NSH = -(-SHF // P)
    NCH = NSH + E * F // P
    NRT = NCH - NSH
    SH_TAIL = SHF - (NSH - 1) * P
    FT = NCH * P
    KW = LO_ROW + E
    assert C == P and E * F % P == 0 and NT * P == SEQ and NCH % 2 == 0 and E == 8

    xv = x.rearrange("b (i p) c -> b p i c", p=P)
    ov = out.rearrange("b (i p) c -> b p i c", p=P)

    with ExitStack() as ctx:
        def sb(name, shape, dt=F32):
            return ctx.enter_context(nc.sbuf_tensor(name, shape, dt))

        def sem(name):
            return ctx.enter_context(nc.semaphore(name))

        bank = [ctx.enter_context(nc.psum_tensor(f"bank{i}", [P, 512], F32)) for i in range(8)]
        ps_score = bank[0:2]
        ps_pT = bank[2:4]
        ps_qk, ps_v, ps_y, ps_x1 = bank[4], bank[5], bank[6], bank[7]
        ps_gate, ps_up, ps_w = bank[0:2], bank[2:4], bank[4:6]
        ps_down, ps_out = bank[6], bank[7]

        x_tok = sb("x_tok", [P, NB * NT, C + 2])
        xT_h = sb("xT_h", [P, NTOK], F32R)
        xT_l = sb("xT_l", [P, NTOK], F32R)
        xv_h = sb("xv_h", [P, SEQ], F32R)
        xv_l = sb("xv_l", [P, SEQ], F32R)
        Wm = sb("Wm", [P, NJ, C])
        WmT = sb("WmT", [P, D3])
        WqkT_h = sb("WqkT_h", [P, 2 * C], F32R)
        WqkT_l = sb("WqkT_l", [P, 2 * C], F32R)
        loA = sb("loA", [P, R])
        loB = sb("loB", [R, D3])
        loAT = sb("loAT", [R, P])
        pA = sb("pA", [P, R])
        pB = sb("pB", [R, C])
        pAT = sb("pAT", [R, P])
        Wp = sb("Wp", [P, C])
        Wmp = sb("Wmp", [P, C])
        WmpT = sb("WmpT", [P, C])
        W2T = sb("W2T", [P, C])
        W2s = sb("W2s", [P, C])
        Wv = sb("Wv", [P, C])
        WvoT_h = sb("WvoT_h", [P, C], F32R)
        WvoT_l = sb("WvoT_l", [P, C], F32R)
        gram = sb("gram", [P, C + 2])
        wgw = sb("wgw", [P, D3])
        bn_rows = sb("bn_rows", [2 * NJ, C])
        bn_cols = sb("bn_cols", [P, 2 * NJ])
        mean = sb("mean", [P, NJ])
        msq = sb("msq", [P, NJ])
        var = sb("var", [P, NJ])
        rstd = sb("rstd", [P, NJ])
        bn_s = sb("bn_s", [P, NJ])
        bn_t = sb("bn_t", [P, NJ])
        mst = sb("mst", [P, NJ])
        qk_s = sb("qk_s", [P, 2])
        qk_t = sb("qk_t", [P, 2])
        tv_b = sb("tv_b", [P, P])
        bias_tok = sb("bias_tok", [P, C])
        x_res = sb("x_res", [P, NT, C])
        qf = sb("qf", [P, SEQ])
        kf = sb("kf", [P, SEQ])
        q_h = sb("q_h", [P, SEQ], F32R)
        q_l = sb("q_l", [P, SEQ], F32R)
        k_h = sb("k_h", [P, SEQ], F32R)
        k_l = sb("k_l", [P, SEQ], F32R)
        v_h = sb("v_h", [P, NT, C], F32R)
        v_l = sb("v_l", [P, NT, C], F32R)
        negmax = sb("negmax", [P, NT])
        rowsum = sb("rowsum", [P, NT])
        rinv = sb("rinv", [P, NT])
        prob = sb("prob", [P, 2, SEQ])
        pT_h = sb("pT_h", [P, 2, SEQ], F32R)
        pT_l = sb("pT_l", [P, 2, SEQ], F32R)
        res1 = sb("res1", [P, NT, C])
        stats = sb("stats", [P, NT, 6])
        mv = sb("mv", [P, NT, 2])
        veps = sb("veps", [P, NT])
        lrstd = sb("lrstd", [P, NT])
        x1cur = sb("x1cur", [P, NT, C])
        x1_all = sb("x1_all", [P, NB * NT, C])
        x1T_h = sb("x1T_h", [P, SEQ], F32R)
        x1T_l = sb("x1T_l", [P, SEQ], F32R)
        x1Ta_h = sb("x1Ta_h", [P, NTOK], F32R)
        x1Ta_l = sb("x1Ta_l", [P, NTOK], F32R)
        gw = sb("gw", [P, E])
        gw_h = sb("gw_h", [P, E], F32R)
        gw_l = sb("gw_l", [P, E], F32R)
        logit = sb("logit", [P, NT, 2 * E])
        top8 = sb("top8", [P, NT, 8])
        pick = sb("pick", [P, NT, 8])
        marked = sb("marked", [P, NT, 2 * E])
        chosen = sb("chosen", [P, NT, E])
        ldiff = sb("ldiff", [P, NT, E])
        lexp = sb("lexp", [P, NT, E])
        wsum = sb("wsum", [P, NT])
        winv = sb("winv", [P, NT])
        wfull = sb("wfull", [P, NT, E])
        wpad = sb("wpad", [P, NT, P])
        wround = sb("wround", [P, NT, E], F32R)
        wT = sb("wT", [KW, NTOK], F32R)
        sel_f = sb("sel_f", [KW, E * F])
        sel = sb("sel", [KW, E * F], F32R)
        Wg_raw = sb("Wg_raw", [P, FT])
        Wu_raw = sb("Wu_raw", [P, FT])
        Wd_raw = sb("Wd_raw", [P, NCH, C])
        Wg_h = sb("Wg_h", [P, FT], F32R)
        Wg_l = sb("Wg_l", [P, FT], F32R)
        Wu_h = sb("Wu_h", [P, FT], F32R)
        Wu_l = sb("Wu_l", [P, FT], F32R)
        Wd_h = sb("Wd_h", [P, NCH, C], F32R)
        Wd_l = sb("Wd_l", [P, NCH, C], F32R)
        silu = [qf, kf]
        su = [prob[:, 0], prob[:, 1]]
        hid = [sb("hid0", [P, SEQ]), x_res[:].rearrange("p i c -> p (i c)")]
        hT_h = [q_h[:], k_h[:]]
        hT_l = [q_l[:], k_l[:]]
        y_sb = sb("y_sb", [P, SEQ])
        r2 = sb("r2", [P, NT, C])
        o_tok = sb("o_tok", [P, NT, C])
        ident = sb("ident", [P, P])
        ident_r = sb("ident_r", [P, P], F32R)
        mask_f = sb("mask_f", [P, P])
        mask_r = sb("mask_r", [P, P], F32R)
        ones = sb("ones", [P, P])
        nhalf = sb("nhalf", [P, NT])

        x_in, wa_in, lora_in, wp_in, bn_in, gw_in = map(sem, ("x_in", "wa_in", "lora_in", "wp_in", "bn_in", "gw_in"))
        wg_in, wu_in, wd_in = map(sem, ("wg_in", "wu_in", "wd_in"))
        xv_in, x1_kept, out_stored = map(sem, ("xv_in", "x1_kept", "out_stored"))
        pool_const = sem("pool_const")
        dve_const = sem("dve_const")
        names = ("loraAT_pe loraAT_sb lora_pe wm_sb xT_pe xTh_sb xTl_sb wmT_pe wmT_sb wmpT_pe wmpT_sb gram_pe gram_sb "
                 "w2_pe w2_sb gw_pe wgw_sb moments_pe bn_var bn_rstd bn_ready w2s_sb wvo_pe wvoh_sb wvol_sb bias_pe "
                 "bias_sb tvb_sb wqkh_sb wqkl_sb gwh_sb gwl_sb").split()
        ss = {n: sem(n) for n in names}
        dve_step = sem("dve_step")
        names = ("qk_pe qk_sb qkh_sb qkl_sb v_pe vh_sb vl_sb score_pe max_sb prob_sb pT_pe pTh_sb pTl_sb y_pe "
                 "xres_sb res_free lnvar_sb lnrstd_sb x1_sb x1T_pe x1Th_sb x1Tl_sb logit_pe ldiff_sb lexp_sb "
                 "wpad_sb wT_pe wT_sb").split()
        sa = {n: sem(n) for n in names}
        names = ("wsplit_h wsplit_l gate_pe gate_free up_pe up_free w_pe w_free silu_sb su_sb hid_sb hTh_sb hTl_sb "
                 "down_pe y_done y_sbd yT_pe r2_sb ln2var_sb ln2rstd_sb o_sb").split()
        sf = {n: sem(n) for n in names}

        block = ctx.enter_context(nc.Block())

        CONST_ONES, CONST_PAD, CONST_IDENT, CONST_MASK, CONST_FILL, CONST_SEL = 1, 2, 4, 5, 6, 13

        def blk(i):
            return slice(i * P, (i + 1) * P)

        @block.sync
        def _(sp):
            sp.wait_ge(pool_const, CONST_ONES)
            for b in range(NB):
                sp.dma_start(x_tok[:, b * NT:(b + 1) * NT, 0:C], xv[b]).then_inc(x_in, 16)
            sp.dma_start(gw[:], gate_w).then_inc(gw_in, 16)
            sp.wait_ge(pool_const, CONST_PAD)
            for raw, shared, routed, done in ((Wg_raw, sh_gate, exp_gate, wg_in), (Wu_raw, sh_up, exp_up, wu_in)):
                sp.dma_start(raw[:, 0:SHF].rearrange("c (s f) -> c s f", s=S),
                             shared.rearrange("s c f -> c s f")).then_inc(done, 16)
                sp.dma_start(raw[:, NSH * P:FT].rearrange("c (e f) -> c e f", e=E),
                             routed.rearrange("e c f -> c e f")).then_inc(done, 16)
            shd = sh_down.rearrange("s f c -> (s f) c")
            sp.dma_start(Wd_raw[:, 0:NSH - 1, :],
                         shd[0:(NSH - 1) * P].rearrange("(k p) c -> p k c", p=P)).then_inc(wd_in, 16)
            sp.dma_start(Wd_raw[0:SH_TAIL, NSH - 1, :], shd[(NSH - 1) * P:SHF]).then_inc(wd_in, 16)
            sp.dma_start(Wd_raw[:, NSH:NCH, :],
                         exp_down.rearrange("e f c -> (e f) c").rearrange("(k p) c -> p k c", p=P)).then_inc(wd_in, 16)

            def keep_x1(b):
                need(sp, x1_kept, 48 * b)
                sp.wait_ge(sa["x1_sb"], b + 1)
                sp.dma_start(x1_all[:, bass.ds(b * NT, NT), :], x1cur[:]).then_inc(x1_kept, 16)
                sp.wait_ge(sa["x1Tl_sb"], b + 1)
                sp.dma_start(x1Ta_h[:, bass.ds(b * SEQ, SEQ)].bitcast(F32), x1T_h[:].bitcast(F32)).then_inc(x1_kept, 16)
                sp.dma_start(x1Ta_l[:, bass.ds(b * SEQ, SEQ)].bitcast(F32), x1T_l[:].bitcast(F32)).then_inc(x1_kept, 16)

            def fetch_xv(b):
                need(sp, xv_in, 32 * b)
                need(sp, sa["v_pe"], b)
                sp.dma_start(xv_h[:].bitcast(F32), xT_h[:, bass.ds(b * SEQ, SEQ)].bitcast(F32)).then_inc(xv_in, 16)
                sp.dma_start(xv_l[:].bitcast(F32), xT_l[:, bass.ds(b * SEQ, SEQ)].bitcast(F32)).then_inc(xv_in, 16)

            def store(g):
                need(sp, out_stored, 16 * g)
                sp.wait_ge(sf["o_sb"], g + 1)
                sp.dma_start(ov[g], o_tok[:]).then_inc(out_stored, 16)

            sp.wait_ge(ss["xTl_sb"], NB)
            fetch_xv(0)
            fetch_xv(1)
            keep_x1(0)
            with sp.Fori(2, NB) as b:
                fetch_xv(b)
                keep_x1(b - 1)
            keep_x1(NB - 1)
            for g in range(NB):
                store(g)
            sp.wait_ge(out_stored, 16 * NB)

        @block.gpsimd
        def _(pool):
            made = [0]

            def const(ins):
                made[0] += 1
                ins.then_inc(pool_const, 1)
                pool.wait_ge(pool_const, made[0])

            g = nc.gpsimd
            const(g.memset(x_tok[:, :, C:C + 2], 1.0))
            g.memset(Wg_raw[:, SHF:NSH * P], 0.0)
            g.memset(Wu_raw[:, SHF:NSH * P], 0.0)
            const(g.memset(Wd_raw[:, NSH - 1, :], 0.0))
            g.memset(ones[:], 1.0)
            g.memset(nhalf[:], -0.5)
            const(g.memset(mask_f[:], 0.0))
            const(g.affine_select(out=ident[:], in_=ones[:], compare_op=ALU.is_equal, fill=0.0, base=0,
                                  pattern=[[-1, P]], channel_multiplier=1))
            const(g.affine_select(out=mask_f[:], in_=mask_f[:], compare_op=ALU.is_ge, fill=MASKED, base=0,
                                  pattern=[[-1, P]], channel_multiplier=1))
            g.memset(logit[:], BIG)
            g.memset(pick[:], BIG)
            const(g.memset(wpad[:], 0.0))
            const(g.memset(sel_f[:], 0.0))
            for row in (0, LO_ROW):
                part = sel_f[row:row + E, :]
                const(g.memset(part, 1.0))
                const(g.affine_select(out=part, in_=part, compare_op=ALU.is_ge, fill=0.0, base=0,
                                      pattern=[[1, E * F]], channel_multiplier=-F))
                const(g.affine_select(out=part, in_=part, compare_op=ALU.is_ge, fill=0.0, base=F - 1,
                                      pattern=[[-1, E * F]], channel_multiplier=F))
            assert made[0] == CONST_SEL
            pool.wait_ge(ss["bn_var"], 1)
            nc.gpsimd.tensor_tensor(out=rstd[:], in0=var[:], in1=nhalf[:, 0:NJ], op=ALU.pow).then_inc(ss["bn_rstd"], 1)

            def split_qk(b):
                for n, (full, hi, lo) in enumerate(((qf, q_h, q_l), (kf, k_h, k_l))):
                    pool.wait_ge(sa["qkh_sb"], 2 * b + n + 1)
                    nc.gpsimd.tensor_tensor(out=lo[:], in0=full[:], in1=hi[:].bitcast(F32),
                                            op=ALU.subtract).then_inc(sa["qkl_sb"], 1)

            def residual_base(b):
                need(pool, sa["res_free"], b)
                nc.gpsimd.tensor_tensor(out=x_res[:], in0=x_tok[:, bass.ds(b * NT, NT), 0:C],
                                        in1=bias_tok[:].unsqueeze(1).broadcast_to((P, NT, C)),
                                        op=ALU.add).then_inc(sa["xres_sb"], 1)

            def ln_rstd(b):
                pool.wait_ge(sa["lnvar_sb"], b + 1)
                nc.gpsimd.tensor_tensor(out=lrstd[:], in0=veps[:], in1=nhalf[:], op=ALU.pow).then_inc(sa["lnrstd_sb"], 1)

            def split_weight(n, raw, hi, lo):
                pool.wait_ge(sf["wsplit_h"], n + 1)
                nc.gpsimd.tensor_tensor(out=lo, in0=raw, in1=hi.bitcast(F32), op=ALU.subtract).then_inc(sf["wsplit_l"], 1)

            pool.wait_ge(ss["bias_sb"], 1)
            split_qk(0)
            residual_base(0)
            split_weight(0, Wg_raw[:], Wg_h[:], Wg_l[:])
            split_qk(1)
            ln_rstd(0)
            with pool.Fori(1, NB - 1) as b:
                residual_base(b)
                split_qk(b + 1)
                ln_rstd(b)
            residual_base(NB - 1)
            split_weight(1, Wu_raw[:], Wu_h[:], Wu_l[:])
            ln_rstd(NB - 1)
            split_weight(2, Wd_raw[:], Wd_h[:], Wd_l[:])

            def split_hidden(g, j):
                n = g * NCH + j
                pool.wait_ge(sf["hTh_sb"], n + 1)
                nc.gpsimd.tensor_tensor(out=hT_l[j % 2], in0=hid[j % 2][:], in1=hT_h[j % 2].bitcast(F32),
                                        op=ALU.subtract).then_inc(sf["hTl_sb"], 1)

            def ln2_rstd(g):
                pool.wait_ge(sf["ln2var_sb"], g + 1)
                nc.gpsimd.tensor_tensor(out=lrstd[:], in0=veps[:], in1=nhalf[:], op=ALU.pow).then_inc(sf["ln2rstd_sb"], 1)

            for j in range(NCH):
                split_hidden(0, j)
            with pool.Fori(1, NB) as g:
                for j in range(NCH):
                    split_hidden(g, j)
                    if j == 7:
                        ln2_rstd(g - 1)
            ln2_rstd(NB - 1)

        @block.tensor
        def _(pe):
            def mm3(dst, lh, ll, rh, rl, start=True, stop=True, skip=False):
                nc.tensor.matmul(dst, lh, rh, start=start, stop=False, skip_group_check=skip)
                nc.tensor.matmul(dst, lh, rl, start=False, stop=False, skip_group_check=skip)
                return nc.tensor.matmul(dst, ll, rh, start=False, stop=stop, skip_group_check=skip)

            pe.wait_ge(pool_const, CONST_IDENT)
            pe.wait_ge(lora_in, 64)
            nc.tensor.transpose(bank[0][0:R, 0:P], loA[:], ident[:])
            nc.tensor.transpose(bank[0][0:R, P:2 * P], pA[:], ident[:]).then_inc(ss["loraAT_pe"], 1)
            pe.wait_ge(ss["loraAT_sb"], 1)
            nc.tensor.matmul(bank[1][:, 0:D3], loAT[:], loB[:], start=True, stop=True).then_inc(ss["lora_pe"], 1)
            nc.tensor.matmul(bank[2][:, 0:C], pAT[:], pB[:], start=True, stop=True).then_inc(ss["lora_pe"], 1)
            pe.wait_ge(x_in, 16 * NB)
            for b in range(NB):
                for i in range(NT):
                    last = nc.tensor.transpose(bank[4 + b][:, blk(i)], x_tok[:, b * NT + i, 0:C], ident[:])
                last.then_inc(ss["xT_pe"], 1)
            pe.wait_ge(ss["wm_sb"], 2)
            for j in range(NJ):
                last = nc.tensor.transpose(bank[0][:, blk(j)], Wm[:, j, :], ident[:])
            last.then_inc(ss["wmT_pe"], 1)
            nc.tensor.transpose(bank[2][:, 0:C], Wmp[:], ident[:]).then_inc(ss["wmpT_pe"], 1)
            for t in range(NB * NT):
                last = nc.tensor.matmul(bank[3][:, 0:C + 1], x_tok[:, t, 0:C], x_tok[:, t, 0:C + 1],
                                        start=(t == 0), stop=(t == NB * NT - 1))
            last.then_inc(ss["gram_pe"], 1)
            pe.wait_ge(ss["wmpT_sb"], 1)
            nc.tensor.matmul(bank[2][:, P:2 * P], Wp[:], WmpT[:], start=True, stop=True).then_inc(ss["w2_pe"], 1)
            pe.wait_ge(ss["gram_sb"], 1)
            pe.wait_ge(ss["wmT_sb"], 1)
            nc.tensor.matmul(bank[1][:, 0:D3], gram[:, 0:C], WmT[:], start=True, stop=True).then_inc(ss["gw_pe"], 1)
            nc.tensor.transpose(bank[0][:, 0:C], WmT[:, 2 * C:3 * C], ident[:])
            pe.wait_ge(bn_in, 32)
            nc.tensor.transpose(bank[0][:, P:P + 2 * NJ], bn_rows[:], ident[0:2 * NJ, 0:2 * NJ])
            pe.wait_ge(ss["wgw_sb"], 1)
            for j in range(NJ):
                nc.tensor.matmul(bank[0][:, 160 + j:161 + j], wgw[:, blk(j)], ones[:, 0:1], start=True, stop=True)
                last = nc.tensor.matmul(bank[0][:, 176 + j:177 + j], WmT[:, blk(j)], gram[:, C:C + 1],
                                        start=True, stop=True)
            last.then_inc(ss["moments_pe"], 1)
            pe.wait_ge(ss["w2s_sb"], 1)
            nc.tensor.matmul(bank[1][:, 0:C], Wv[:], W2s[:], start=True, stop=True).then_inc(ss["wvo_pe"], 1)
            pe.wait_ge(ss["tvb_sb"], 1)
            nc.tensor.matmul(bank[3][:, 0:C], tv_b[:], W2T[:], start=True, stop=True).then_inc(ss["bias_pe"], 1)

            def project_qk(b, n):
                if n == 0:
                    need(pe, sa["qk_sb"], 2 * b)
                else:
                    pe.wait_ge(sa["qk_sb"], 2 * b + 1)
                mm3(ps_qk[:], WqkT_h[:, blk(n)], WqkT_l[:, blk(n)], xT_h[:, bass.ds(b * SEQ, SEQ)],
                    xT_l[:, bass.ds(b * SEQ, SEQ)]).then_inc(sa["qk_pe"], 1)

            def project_v(b):
                pe.wait_ge(xv_in, 32 * b + 32)
                need(pe, sa["vl_sb"], b)
                for i in range(NT):
                    last = mm3(ps_v[:, blk(i)], xv_h[:, blk(i)], xv_l[:, blk(i)], WvoT_h[:], WvoT_l[:])
                last.then_inc(sa["v_pe"], 1)

            def scores(b, i):
                t = NT * b + i
                if i == 0:
                    pe.wait_ge(sa["qkl_sb"], 2 * b + 2)
                need(pe, sa["prob_sb"], t - 1)
                w = (i + 1) * P
                dst = ps_score[i % 2]
                mm3(dst[:, 0:w], q_h[:, blk(i)], q_l[:, blk(i)], k_h[:, 0:w], k_l[:, 0:w], stop=False)
                nc.tensor.matmul(dst[:, blk(i)], ident_r[:], mask_r[:], start=False, stop=True).then_inc(sa["score_pe"], 1)

            def transpose_probs(b, i):
                t = NT * b + i
                pe.wait_ge(sa["prob_sb"], t + 1)
                need(pe, sa["pTl_sb"], t - 1)
                for j in range(i + 1):
                    last = nc.tensor.transpose(ps_pT[i % 2][:, blk(j)], prob[:, i % 2, blk(j)], ident[:])
                last.then_inc(sa["pT_pe"], 1)

            def attend(b, i):
                t = NT * b + i
                if i == 0:
                    pe.wait_ge(sa["vl_sb"], b + 1)
                    need(pe, sa["res_free"], b)
                pe.wait_ge(sa["pTl_sb"], t + 1)
                for j in range(i + 1):
                    last = mm3(ps_y[:, blk(i)], pT_h[:, i % 2, blk(j)], pT_l[:, i % 2, blk(j)], v_h[:, j, :], v_l[:, j, :],
                               start=(j == 0), stop=(j == i))
                last.then_inc(sa["y_pe"], 1)

            def transpose_x1(b):
                pe.wait_ge(sa["x1_sb"], b + 1)
                need(pe, sa["wT_sb"], b)
                for i in range(NT):
                    last = nc.tensor.transpose(ps_x1[:, blk(i)], x1cur[:, i, :], ident[:])
                last.then_inc(sa["x1T_pe"], 1)

            def logits(b):
                pe.wait_ge(sa["x1Tl_sb"], b + 1)
                for i in range(NT):
                    last = mm3(ps_x1[:, i * E:(i + 1) * E], x1T_h[:, blk(i)], x1T_l[:, blk(i)], gw_h[:], gw_l[:])
                last.then_inc(sa["logit_pe"], 1)

            def transpose_w(b):
                pe.wait_ge(sa["wpad_sb"], b + 1)
                for i in range(NT):
                    last = nc.tensor.transpose(ps_x1[:, blk(i)], wpad[:, i, :], ident[:])
                last.then_inc(sa["wT_pe"], 1)

            def attention(b, first=False, last=False):
                scores(b, 0)
                scores(b, 1)
                project_v(b)
                if not first:
                    transpose_x1(b - 1)
                transpose_probs(b, 0)
                scores(b, 2)
                if not first:
                    logits(b - 1)
                attend(b, 0)
                transpose_probs(b, 1)
                scores(b, 3)
                attend(b, 1)
                transpose_probs(b, 2)
                if not first:
                    transpose_w(b - 1)
                if not last:
                    project_qk(b + 1, 0)
                attend(b, 2)
                transpose_probs(b, 3)
                if not last:
                    project_qk(b + 1, 1)
                attend(b, 3)

            pe.wait_ge(ss["xTl_sb"], NB)
            pe.wait_ge(ss["wqkl_sb"], 1)
            project_qk(0, 0)
            project_qk(0, 1)
            pe.wait_ge(ss["wvol_sb"], 1)
            pe.wait_ge(ss["bias_sb"], 1)
            pe.wait_ge(dve_const, 2)
            pe.wait_ge(ss["gwl_sb"], 1)
            attention(0, first=True)
            with pe.Fori(1, NB - 1) as b:
                attention(b)
            attention(NB - 1, last=True)
            transpose_x1(NB - 1)
            logits(NB - 1)
            transpose_w(NB - 1)

            def up_chunk(g, j):
                n = g * NCH + j
                xh, xl = x1Ta_h[:, bass.ds(g * SEQ, SEQ)], x1Ta_l[:, bass.ds(g * SEQ, SEQ)]
                need(pe, sf["silu_sb"], n - 1)
                mm3(ps_gate[j % 2][:], Wg_h[:, blk(j)], Wg_l[:, blk(j)], xh, xl).then_inc(sf["gate_pe"], 1)
                need(pe, sf["su_sb"], n - 1)
                if j >= NSH:
                    need(pe, sf["hid_sb"], g * NRT + max(0, j - NSH - 1))
                mm3(ps_up[j % 2][:], Wu_h[:, blk(j)], Wu_l[:, blk(j)], xh, xl).then_inc(sf["up_pe"], 1)
                if j >= NSH:
                    c = j - NSH
                    nc.tensor.matmul(ps_w[j % 2][:], sel[:, blk(c)], wT[:, bass.ds(g * SEQ, SEQ)],
                                     start=True, stop=True).then_inc(sf["w_pe"], 1)

            def down_chunk(g, j):
                n = g * NCH + j
                if j == 0:
                    need(pe, sf["y_sbd"], g)
                pe.wait_ge(sf["hTl_sb"], n + 1)
                mm3(ps_down[:], Wd_h[:, j, :], Wd_l[:, j, :], hT_h[j % 2], hT_l[j % 2],
                    start=(j == 0), stop=(j == NCH - 1)).then_inc(sf["down_pe"], 1)

            def transpose_y(g):
                pe.wait_ge(sf["y_sbd"], g + 1)
                need(pe, sf["r2_sb"], g)
                for i in range(NT):
                    last = nc.tensor.transpose(ps_out[:, blk(i)], y_sb[:, blk(i)], ident[:])
                last.then_inc(sf["yT_pe"], 1)

            def group(g, first=False):
                for j in range(NCH):
                    up_chunk(g, j)
                    if j >= 2:
                        down_chunk(g, j - 2)
                    elif not first:
                        down_chunk(g - 1, NCH - 2 + j)
                    if j == 3 and not first:
                        transpose_y(g - 1)

            pe.wait_ge(x1_kept, 48 * NB)
            pe.wait_ge(sf["wsplit_l"], 3)
            pe.wait_ge(sa["wT_sb"], NB)
            pe.wait_ge(sa["res_free"], NB)
            group(0, first=True)
            with pe.Fori(1, NB) as g:
                group(g)
            down_chunk(NB - 1, NCH - 2)
            down_chunk(NB - 1, NCH - 1)
            transpose_y(NB - 1)

        @block.scalar
        def _(act):
            act.dma_start(loA[:], attn_A).then_inc(lora_in, 16)
            act.dma_start(loB[:], attn_B).then_inc(lora_in, 16)
            act.dma_start(pA[:], proj_A).then_inc(lora_in, 16)
            act.dma_start(pB[:], proj_B).then_inc(lora_in, 16)
            act.dma_start(Wm[:].rearrange("c j k -> c (j k)"),
                          W_attn.rearrange("(c j) k -> c (j k)", j=NJ)).then_inc(wa_in, 16)
            act.dma_start(Wp[:], W_proj).then_inc(wp_in, 16)
            act.dma_start(bn_rows[0:NJ, :], bn_gamma.rearrange("(j d) -> j d", d=C)).then_inc(bn_in, 16)
            act.dma_start(bn_rows[NJ:2 * NJ, :], bn_beta.rearrange("(j d) -> j d", d=C)).then_inc(bn_in, 16)
            act.preload_act_table(ACT.Exp)

            act.wait_ge(ss["loraAT_pe"], 1)
            nc.scalar.activation(loAT[:], bank[0][0:R, 0:P], ACT.Copy)
            nc.scalar.activation(pAT[:], bank[0][0:R, P:2 * P], ACT.Copy).then_inc(ss["loraAT_sb"], 1)
            for b in range(NB):
                act.wait_ge(ss["xT_pe"], b + 1)
                nc.scalar.activation(xT_h[:, b * SEQ:(b + 1) * SEQ], bank[4 + b][:], ACT.Copy).then_inc(ss["xTh_sb"], 1)
            act.wait_ge(ss["wmT_pe"], 1)
            nc.scalar.activation(WmT[:].rearrange("p (c j) -> p j c", j=NJ),
                                 bank[0][:, 0:D3].rearrange("p (j c) -> p j c", j=NJ), ACT.Copy).then_inc(ss["wmT_sb"], 1)
            act.wait_ge(ss["wmpT_pe"], 1)
            nc.scalar.activation(WmpT[:], bank[2][:, 0:C], ACT.Copy).then_inc(ss["wmpT_sb"], 1)
            act.wait_ge(ss["gram_pe"], 1)
            nc.scalar.activation(gram[:, 0:C + 1], bank[3][:, 0:C + 1], ACT.Copy).then_inc(ss["gram_sb"], 1)
            act.wait_ge(ss["w2_pe"], 1)
            nc.scalar.activation(W2T[:], bank[2][:, P:2 * P], ACT.Copy).then_inc(ss["w2_sb"], 1)
            act.wait_ge(ss["wmT_sb"], 1)
            nc.scalar.activation(WqkT_h[:], WmT[:, 0:2 * C], ACT.Copy).then_inc(ss["wqkh_sb"], 1)

            def affine_qk(b, n):
                act.wait_ge(sa["qk_pe"], 2 * b + n + 1)
                need(act, sa["qkl_sb"], 2 * b - 1 + n)
                full = (qf, kf)[n]
                nc.scalar.activation(full[:], ps_qk[:], ACT.Identity, bias=qk_t[:, n:n + 1],
                                     scale=qk_s[:, n:n + 1]).then_inc(sa["qk_sb"], 1)

            def value_high(b):
                act.wait_ge(sa["v_pe"], b + 1)
                need(act, sa["y_pe"], NT * b)
                nc.scalar.activation(v_h[:].rearrange("p i c -> p (i c)"), ps_v[:], ACT.Copy).then_inc(sa["vh_sb"], 1)

            def probs(b, i):
                t = NT * b + i
                act.wait_ge(sa["max_sb"], t + 1)
                need(act, sa["pT_pe"], t - 1)
                if i == 0:
                    need(act, sa["res_free"], b)
                w = (i + 1) * P
                nc.scalar.activation(prob[:, i % 2, 0:w], ps_score[i % 2][:, 0:w], ACT.Exp, bias=negmax[:, i:i + 1],
                                     accum_out=rowsum[:, i:i + 1]).then_inc(sa["prob_sb"], 1)

            def probsT_high(b, i):
                t = NT * b + i
                act.wait_ge(sa["pT_pe"], t + 1)
                need(act, sa["y_pe"], t - 1)
                w = (i + 1) * P
                nc.scalar.activation(pT_h[:, i % 2, 0:w], ps_pT[i % 2][:, 0:w], ACT.Copy).then_inc(sa["pTh_sb"], 1)

            def x1T_high(b):
                act.wait_ge(sa["x1T_pe"], b + 1)
                need(act, x1_kept, 48 * b)
                need(act, sa["logit_pe"], b)
                nc.scalar.activation(x1T_h[:], ps_x1[:], ACT.Copy).then_inc(sa["x1Th_sb"], 1)

            def router_exp(b):
                act.wait_ge(sa["ldiff_sb"], b + 1)
                nc.scalar.activation(lexp[:], ldiff[:], ACT.Exp).then_inc(sa["lexp_sb"], 1)

            def weight_high(n, raw, hi, arrived, count):
                act.wait_ge(arrived, count)
                nc.scalar.activation(hi, raw, ACT.Copy).then_inc(sf["wsplit_h"], 1)

            def attention(b, first=False, last=False):
                probs(b, 0)
                probs(b, 1)
                value_high(b)
                if not first:
                    x1T_high(b - 1)
                probsT_high(b, 0)
                probs(b, 2)
                probsT_high(b, 1)
                if not first:
                    router_exp(b - 1)
                probs(b, 3)
                probsT_high(b, 2)
                if not last:
                    affine_qk(b + 1, 0)
                probsT_high(b, 3)
                if not last:
                    affine_qk(b + 1, 1)

            act.wait_ge(ss["bn_ready"], 1)
            affine_qk(0, 0)
            affine_qk(0, 1)
            act.wait_ge(ss["wvo_pe"], 1)
            nc.scalar.activation(WvoT_h[:], bank[1][:, 0:C], ACT.Copy).then_inc(ss["wvoh_sb"], 1)
            act.wait_ge(ss["bias_pe"], 1)
            nc.scalar.activation(bias_tok[:], bank[3][:, 0:C], ACT.Copy).then_inc(ss["bias_sb"], 1)
            weight_high(0, Wg_raw[:], Wg_h[:], wg_in, 32)
            attention(0, first=True)
            with act.Fori(1, NB - 1) as b:
                attention(b)
            weight_high(1, Wu_raw[:], Wu_h[:], wu_in, 32)
            attention(NB - 1, last=True)
            weight_high(2, Wd_raw[:], Wd_h[:], wd_in, 48)
            x1T_high(NB - 1)
            router_exp(NB - 1)

            def gate_silu(g, j):
                n = g * NCH + j
                act.wait_ge(sf["gate_pe"], n + 1)
                need(act, sf["su_sb"], n - 1)
                nc.scalar.activation(silu[j % 2][:], ps_gate[j % 2][:], ACT.Silu).then_inc(sf["silu_sb"], 1)

            def hidden_high(g, j):
                n = g * NCH + j
                if j < NSH:
                    act.wait_ge(sf["su_sb"], n + 1)
                else:
                    act.wait_ge(sf["hid_sb"], g * NRT + j - NSH + 1)
                need(act, sf["down_pe"], n - 1)
                nc.scalar.activation(hT_h[j % 2], hid[j % 2][:], ACT.Copy).then_inc(sf["hTh_sb"], 1)

            def down_out(g):
                act.wait_ge(sf["down_pe"], (g + 1) * NCH)
                need(act, sf["yT_pe"], g)
                nc.scalar.activation(y_sb[:], ps_down[:], ACT.Copy).then_inc(sf["y_sbd"], 1)

            act.preload_act_table(ACT.Silu)
            act.wait_ge(sa["y_pe"], NB * NT)
            for j in range(NCH):
                gate_silu(0, j)
                if j >= 1:
                    hidden_high(0, j - 1)
            with act.Fori(1, NB) as g:
                for j in range(NCH):
                    gate_silu(g, j)
                    if j == 0:
                        hidden_high(g - 1, NCH - 1)
                    else:
                        hidden_high(g, j - 1)
                    if j == 2:
                        down_out(g - 1)
            hidden_high(NB - 1, NCH - 1)
            down_out(NB - 1)

        @block.vector
        def _(dve):
            v = nc.vector
            st = Steps(dve, dve_step)
            dve.wait_ge(pool_const, CONST_MASK)
            v.tensor_copy(ident_r[:], ident[:]).then_inc(dve_const, 1)
            v.tensor_copy(mask_r[:], mask_f[:]).then_inc(dve_const, 1)
            dve.wait_ge(ss["lora_pe"], 1)
            dve.wait_ge(wa_in, 16)
            wm_flat = Wm[:].rearrange("c j k -> c (j k)")
            v.tensor_tensor(wm_flat, bank[1][:, 0:D3], wm_flat, ALU.add).then_inc(ss["wm_sb"], 1)
            dve.wait_ge(ss["lora_pe"], 2)
            dve.wait_ge(wp_in, 16)
            v.tensor_tensor(Wmp[:], bank[2][:, 0:C], Wp[:], ALU.add).then_inc(ss["wm_sb"], 1)
            for b in range(NB):
                dve.wait_ge(ss["xTh_sb"], b + 1)
                cols = slice(b * SEQ, (b + 1) * SEQ)
                v.tensor_tensor(xT_l[:, cols], bank[4 + b][:], xT_h[:, cols].bitcast(F32),
                                ALU.subtract).then_inc(ss["xTl_sb"], 1)
            dve.wait_ge(ss["gw_pe"], 1)
            v.tensor_tensor(wgw[:], bank[1][:, 0:D3], WmT[:], ALU.mult).then_inc(ss["wgw_sb"], 1)
            dve.wait_ge(ss["wqkh_sb"], 1)
            v.tensor_tensor(WqkT_l[:], WmT[:, 0:2 * C], WqkT_h[:].bitcast(F32), ALU.subtract).then_inc(ss["wqkl_sb"], 1)
            dve.wait_ge(gw_in, 16)
            v.tensor_copy(gw_h[:], gw[:]).then_inc(ss["gwh_sb"], 1)
            dve.wait_ge(ss["moments_pe"], 1)
            st.done(v.tensor_copy(bn_cols[:], bank[0][:, P:P + 2 * NJ]))
            st.done(v.tensor_copy(Wv[:], bank[0][:, 0:C]))
            st.done(v.tensor_scalar(mean[:], bank[0][:, 176:176 + NJ], 1.0 / NTOK, None, ALU.mult))
            st.wait()
            st.done(v.tensor_tensor(msq[:], mean[:], mean[:], ALU.mult))
            st.wait()
            st.done(v.scalar_tensor_tensor(out=var[:], in0=bank[0][:, 160:160 + NJ], scalar=1.0 / NTOK, in1=msq[:],
                                           op0=ALU.mult, op1=ALU.subtract))
            st.wait()
            v.tensor_scalar(var[:], var[:], 0.0, EPS, ALU.max, ALU.add).then_inc(ss["bn_var"], 1)
            dve.wait_ge(ss["gwh_sb"], 1)
            v.tensor_tensor(gw_l[:], gw[:], gw_h[:].bitcast(F32), ALU.subtract).then_inc(ss["gwl_sb"], 1)
            dve.wait_ge(pool_const, CONST_SEL)
            v.tensor_copy(sel[:], sel_f[:]).then_inc(dve_const, 1)
            dve.wait_ge(ss["bn_rstd"], 1)
            st.done(v.tensor_tensor(bn_s[:], rstd[:], bn_cols[:, 0:NJ], ALU.mult))
            st.wait()
            st.done(v.tensor_tensor(mst[:], mean[:], bn_s[:], ALU.mult))
            st.wait()
            st.done(v.tensor_tensor(bn_t[:], bn_cols[:, NJ:2 * NJ], mst[:], ALU.subtract))
            st.wait()
            v.tensor_scalar(qk_s[:, 0:1], bn_s[:, 0:1], SCALE, None, ALU.mult)
            v.tensor_copy(qk_s[:, 1:2], bn_s[:, 1:2])
            v.tensor_scalar(qk_t[:, 0:1], bn_t[:, 0:1], SCALE, None, ALU.mult)
            v.tensor_copy(qk_t[:, 1:2], bn_t[:, 1:2]).then_inc(ss["bn_ready"], 1)
            dve.wait_ge(ss["w2_sb"], 1)
            v.tensor_scalar(W2s[:], W2T[:], bn_s[:, 2:3], None, ALU.mult).then_inc(ss["w2s_sb"], 1)
            v.tensor_scalar(tv_b[:], ones[:], bn_t[:, 2:3], None, ALU.mult).then_inc(ss["tvb_sb"], 1)

            def qk_high(b, n):
                dve.wait_ge(sa["qk_sb"], 2 * b + n + 1)
                need(dve, sa["score_pe"], NT * b)
                full, hi = ((qf, q_h), (kf, k_h))[n]
                v.tensor_copy(hi[:], full[:]).then_inc(sa["qkh_sb"], 1)

            def value_low(b):
                dve.wait_ge(sa["vh_sb"], b + 1)
                v.tensor_tensor(v_l[:].rearrange("p i c -> p (i c)"), ps_v[:],
                                v_h[:].rearrange("p i c -> p (i c)").bitcast(F32), ALU.subtract).then_inc(sa["vl_sb"], 1)

            def row_max(b, i):
                dve.wait_ge(sa["score_pe"], NT * b + i + 1)
                need(dve, sa["prob_sb"], NT * (b - 1) + i + 1)
                v.tensor_reduce(negmax[:, i:i + 1], ps_score[i % 2][:, 0:(i + 1) * P], AX.X, ALU.max,
                                negate=True).then_inc(sa["max_sb"], 1)

            def probsT_low(b, i):
                dve.wait_ge(sa["pTh_sb"], NT * b + i + 1)
                w = (i + 1) * P
                v.tensor_tensor(pT_l[:, i % 2, 0:w], ps_pT[i % 2][:, 0:w], pT_h[:, i % 2, 0:w].bitcast(F32),
                                ALU.subtract).then_inc(sa["pTl_sb"], 1)

            def row_stats(steps, src, var_ready):
                for i in range(NT):
                    v.bn_stats(stats[:, i, :], src[:, i, :])
                dve.drain()
                for i in range(NT):
                    steps.done(v.bn_aggr(mv[:, i, :], stats[:, i, :]))
                steps.wait()
                v.tensor_scalar(veps[:], mv[:, :, 1], EPS, None, ALU.add).then_inc(var_ready, 1)

            def residual(b, steps):
                dve.wait_ge(sa["prob_sb"], NT * b + NT)
                steps.done(v.reciprocal(rinv[:], rowsum[:]))
                dve.wait_ge(sa["y_pe"], NT * b + NT)
                dve.wait_ge(sa["xres_sb"], b + 1)
                steps.wait()
                for i in range(NT):
                    ins = v.scalar_tensor_tensor(out=res1[:, i, :], in0=ps_y[:, blk(i)], scalar=rinv[:, i:i + 1],
                                                 in1=x_res[:, i, :], op0=ALU.mult, op1=ALU.add)
                ins.then_inc(sa["res_free"], 1)
                dve.wait_ge(sa["res_free"], b + 1)
                row_stats(steps, res1, sa["lnvar_sb"])

            def normalise(b):
                dve.wait_ge(sa["lnrstd_sb"], b + 1)
                need(dve, sa["x1T_pe"], b)
                need(dve, x1_kept, 48 * b)
                for i in range(NT):
                    ins = v.tensor_scalar(x1cur[:, i, :], res1[:, i, :], mv[:, i, 0:1], lrstd[:, i:i + 1],
                                          ALU.subtract, ALU.mult)
                ins.then_inc(sa["x1_sb"], 1)

            def x1T_low(b):
                dve.wait_ge(sa["x1Th_sb"], b + 1)
                v.tensor_tensor(x1T_l[:], ps_x1[:], x1T_h[:].bitcast(F32), ALU.subtract).then_inc(sa["x1Tl_sb"], 1)

            def route_top2(b, steps):
                dve.wait_ge(sa["logit_pe"], b + 1)
                v.tensor_copy(logit[:, :, 0:E], ps_x1[:, 0:NT * E].rearrange("p (i e) -> p i e", e=E))
                dve.drain()
                for i in range(NT):
                    steps.done(v.max(top8[:, i, :], logit[:, i, 0:E]))
                steps.wait()
                v.tensor_tensor(ldiff[:], logit[:, :, 0:E], top8[:, :, 0:1].broadcast_to((P, NT, E)),
                                ALU.subtract).then_inc(sa["ldiff_sb"], 1)
                v.tensor_copy(pick[:, :, 0:2], top8[:, :, 0:2])
                dve.drain()
                for i in range(NT):
                    steps.done(v.match_replace(marked[:, i, 0:E + 6], pick[:, i, :], logit[:, i, 0:E + 6], -BIG))
                steps.wait()
                steps.done(v.tensor_tensor(chosen[:], marked[:, :, 0:E], logit[:, :, 0:E], ALU.not_equal))

            def route_weights(b, steps):
                steps.wait()
                dve.wait_ge(sa["lexp_sb"], b + 1)
                steps.done(v.tensor_tensor(chosen[:], chosen[:], lexp[:], ALU.mult))
                steps.wait()
                steps.done(v.tensor_reduce(wsum[:], chosen[:], AX.X, ALU.add))
                steps.wait()
                steps.done(v.reciprocal(winv[:], wsum[:]))
                steps.wait()
                steps.done(v.tensor_tensor(wfull[:], chosen[:], winv[:].unsqueeze(2).broadcast_to((P, NT, E)), ALU.mult))
                steps.wait()
                steps.done(v.tensor_copy(wround[:], wfull[:]))
                steps.wait()
                v.tensor_copy(wpad[:, :, 0:E], wround[:].bitcast(F32))
                v.tensor_tensor(wpad[:, :, LO_ROW:KW], wfull[:], wround[:].bitcast(F32),
                                ALU.subtract).then_inc(sa["wpad_sb"], 1)

            def keep_weights(b):
                dve.wait_ge(sa["wT_pe"], b + 1)
                v.tensor_copy(wT[:, bass.ds(b * SEQ, SEQ)], ps_x1[0:KW, :]).then_inc(sa["wT_sb"], 1)

            def attention(b, steps, first=False, last=False):
                row_max(b, 0)
                row_max(b, 1)
                if not first:
                    normalise(b - 1)
                value_low(b)
                if not first:
                    x1T_low(b - 1)
                probsT_low(b, 0)
                row_max(b, 2)
                if not first:
                    route_top2(b - 1, steps)
                probsT_low(b, 1)
                row_max(b, 3)
                if not first:
                    route_weights(b - 1, steps)
                probsT_low(b, 2)
                if not first:
                    keep_weights(b - 1)
                if not last:
                    qk_high(b + 1, 0)
                probsT_low(b, 3)
                if not last:
                    qk_high(b + 1, 1)
                residual(b, steps)

            qk_high(0, 0)
            qk_high(0, 1)
            dve.wait_ge(ss["wvoh_sb"], 1)
            v.tensor_tensor(WvoT_l[:], bank[1][:, 0:C], WvoT_h[:].bitcast(F32), ALU.subtract).then_inc(ss["wvol_sb"], 1)
            attention(0, st, first=True)
            per = (1 + 2 * NT) + 5 + (1 + NT)
            with dve.Fori(1, NB - 1) as b:
                steps = Steps(dve, dve_step, (b - 1) * per + st.n)
                attention(b, steps)
            assert steps.n == per, steps.n
            st.n += per * (NB - 2)
            attention(NB - 1, st, last=True)
            normalise(NB - 1)
            x1T_low(NB - 1)
            route_top2(NB - 1, st)
            route_weights(NB - 1, st)
            keep_weights(NB - 1)

            def times_up(g, j):
                n = g * NCH + j
                dve.wait_ge(sf["silu_sb"], n + 1)
                dve.wait_ge(sf["up_pe"], n + 1)
                if j < NSH:
                    need(dve, sf["hTl_sb"], n - 1)
                    v.tensor_tensor(hid[j % 2][:], ps_up[j % 2][:], silu[j % 2][:], ALU.mult).then_inc(sf["su_sb"], 1)
                else:
                    v.tensor_tensor(su[j % 2], ps_up[j % 2][:], silu[j % 2][:], ALU.mult).then_inc(sf["su_sb"], 1)

            def times_weight(g, j):
                n = g * NCH + j
                if j < NSH:
                    return
                dve.wait_ge(sf["su_sb"], n + 1)
                dve.wait_ge(sf["w_pe"], g * NRT + j - NSH + 1)
                need(dve, sf["hTl_sb"], n - 1)
                v.tensor_tensor(hid[j % 2][:], ps_w[j % 2][:], su[j % 2], ALU.mult).then_inc(sf["hid_sb"], 1)

            def residual2(g):
                dve.wait_ge(sf["yT_pe"], g + 1)
                v.tensor_tensor(r2[:], ps_out[:].rearrange("p (i c) -> p i c", c=C),
                                x1_all[:, bass.ds(g * NT, NT), :], ALU.add).then_inc(sf["r2_sb"], 1)

            def stats2(g, steps):
                dve.wait_ge(sf["r2_sb"], g + 1)
                need(dve, sf["ln2rstd_sb"], g)
                row_stats(steps, r2, sf["ln2var_sb"])

            def normalise2(g):
                dve.wait_ge(sf["ln2rstd_sb"], g + 1)
                need(dve, out_stored, 16 * g)
                for i in range(NT):
                    ins = v.tensor_scalar(o_tok[:, i, :], r2[:, i, :], mv[:, i, 0:1], lrstd[:, i:i + 1],
                                          ALU.subtract, ALU.mult)
                ins.then_inc(sf["o_sb"], 1)

            def group(g, steps, first=False):
                for j in range(NCH):
                    times_up(g, j)
                    times_weight(g, j)
                    if not first:
                        if j == 4:
                            residual2(g - 1)
                        if j == 6:
                            stats2(g - 1, steps)
                        if j == 10:
                            normalise2(g - 1)

            group(0, st, first=True)
            per2 = NT
            with dve.Fori(1, NB) as g:
                steps = Steps(dve, dve_step, (g - 1) * per2 + st.n)
                group(g, steps)
            assert steps.n == per2
            st.n += per2 * (NB - 1)
            residual2(NB - 1)
            stats2(NB - 1, st)
            normalise2(NB - 1)


_INS = ["L0_attn_x", "L0_attn_W_attn", "L0_attn_W_proj", "L0_attn_lora_attn_A", "L0_attn_lora_attn_B",
        "L0_attn_lora_proj_A", "L0_attn_lora_proj_B", "L0_attn_bn_gamma", "L0_attn_bn_beta", "L0_ffn_gate_w",
        "L0_ffn_exp_gate", "L0_ffn_exp_up", "L0_ffn_exp_down", "L0_ffn_sh_gate", "L0_ffn_sh_up", "L0_ffn_sh_down"]


def kernel(**inputs):
    import concourse.bacc as bacc
    from concourse.bass_utils import run_bass_kernel_spmd

    nc = bacc.Bacc("TRN2", target_bir_lowering=False, num_devices=1)
    arrays, args = {}, []
    for name in _INS:
        a = np.ascontiguousarray(inputs[name])
        arrays[f"{name}_dram"] = a
        args.append(nc.dram_tensor(f"{name}_dram", a.shape, mybir.dt.from_np(a.dtype), kind="ExternalInput").ap())
    x = inputs["L0_attn_x"]
    args.append(nc.dram_tensor("out_dram", x.shape, F32, kind="ExternalOutput").ap())
    block_kernel(nc, *args)
    r = run_bass_kernel_spmd(nc, [arrays], core_ids=[0])
    return r.results[0]["out_dram"]
```

```python
from contextlib import ExitStack

import numpy as np

import concourse.bass as bass
from concourse import mybir

ALU = mybir.AluOpType
ACT = mybir.ActivationFunctionType
AX = mybir.AxisListType
F32 = mybir.dt.float32
F32R = mybir.dt.float32r

P = 128
EPS = 1e-5
MASKED = -1.0e30
BIG = 3.0e38
LO_ROW = 32


def need(eng, sem, value, start=0):
    if isinstance(value, int) and value <= 0:
        return
    eng.wait_ge(sem, value + start)


class Steps:

    def __init__(self, eng, sem, base=0):
        self.eng, self.sem, self.base, self.n = eng, sem, base, 0

    def done(self, ins):
        self.n += 1
        ins.then_inc(self.sem, 1)

    def wait(self):
        self.eng.wait_ge(self.sem, self.base + self.n)


def block_kernel(nc, x, W_attn, W_proj, attn_A, attn_B, proj_A, proj_B, bn_gamma, bn_beta,
                 gate_w, exp_gate, exp_up, exp_down, sh_gate, sh_up, sh_down, out):
    NB, SEQ, C = x.shape
    R = attn_A.shape[1]
    D3 = W_attn.shape[0]
    NJ = D3 // C
    E, _, F = exp_gate.shape
    S = sh_gate.shape[0]
    NT = SEQ // P
    NTOK = NB * SEQ
    SCALE = float(C) ** -0.5
    SHF = S * F
    NSH = -(-SHF // P)
    NCH = NSH + E * F // P
    NRT = NCH - NSH
    SH_TAIL = SHF - (NSH - 1) * P
    FT = NCH * P
    KW = LO_ROW + E
    assert C == P and E * F % P == 0 and NT * P == SEQ and NCH % 2 == 0 and E == 8

    xv = x.rearrange("b (i p) c -> b p i c", p=P)
    ov = out.rearrange("b (i p) c -> b p i c", p=P)

    with ExitStack() as ctx:
        def sb(name, shape, dt=F32):
            return ctx.enter_context(nc.sbuf_tensor(name, shape, dt))

        def sem(name):
            return ctx.enter_context(nc.semaphore(name))

        bank = [ctx.enter_context(nc.psum_tensor(f"bank{i}", [P, 512], F32)) for i in range(8)]
        ps_q, ps_k, ps_v = bank[0], bank[1], bank[2]
        ps_score = bank[5:8]
        ps_pT = [bank[3], bank[4], bank[0]]
        ps_y, ps_x1 = bank[1], bank[2]
        ps_gate, ps_up, ps_w = bank[5:7], [bank[7], bank[3]], [bank[4], bank[0]]
        ps_down, ps_out = bank[1], bank[2]
        score_at = [(0, 0), (0, P), (1, 0), (2, 0)]
        prob_off = [i * (i + 1) // 2 * P for i in range(NT + 1)]
        pT_parts = [(0, 2), (2, 1), (3, 1)]

        x_tok = sb("x_tok", [P, NB * NT, C + 2])
        xT_h = sb("xT_h", [P, NTOK], F32R)
        xT_l = sb("xT_l", [P, NTOK], F32R)
        Wm = sb("Wm", [P, NJ, C])
        WmT = sb("WmT", [P, D3])
        WqkT_h = sb("WqkT_h", [P, 2 * C], F32R)
        WqkT_l = sb("WqkT_l", [P, 2 * C], F32R)
        loA = sb("loA", [P, R])
        loB = sb("loB", [R, D3])
        loAT = sb("loAT", [R, P])
        pA = sb("pA", [P, R])
        pB = sb("pB", [R, C])
        pAT = sb("pAT", [R, P])
        Wp = sb("Wp", [P, C])
        Wmp = sb("Wmp", [P, C])
        WmpT = sb("WmpT", [P, C])
        W2T = sb("W2T", [P, C])
        W2s = sb("W2s", [P, C])
        Wv = sb("Wv", [P, C])
        WvoT_h = sb("WvoT_h", [P, C], F32R)
        WvoT_l = sb("WvoT_l", [P, C], F32R)
        gram = sb("gram", [P, C + 2])
        wgw = sb("wgw", [P, D3])
        bn_rows = sb("bn_rows", [2 * NJ, C])
        bn_cols = sb("bn_cols", [P, 2 * NJ])
        mean = sb("mean", [P, NJ])
        msq = sb("msq", [P, NJ])
        var = sb("var", [P, NJ])
        rstd = sb("rstd", [P, NJ])
        bn_s = sb("bn_s", [P, NJ])
        bn_t = sb("bn_t", [P, NJ])
        mst = sb("mst", [P, NJ])
        qk_s = sb("qk_s", [P, 2])
        qk_t = sb("qk_t", [P, 2])
        tv_b = sb("tv_b", [P, P])
        bias_tok = sb("bias_tok", [P, C])
        x_res = sb("x_res", [P, NT, C])
        q_all = sb("q_all", [P, NTOK + SEQ])
        kf = sb("kf", [P, SEQ])
        q_h = sb("q_h", [P, SEQ], F32R)
        q_l = sb("q_l", [P, SEQ], F32R)
        k_h = sb("k_h", [P, NTOK], F32R)
        k_l = sb("k_l", [P, NTOK], F32R)
        v_h = sb("v_h", [P, NB * NT, C], F32R)
        v_l = sb("v_l", [P, NB * NT, C], F32R)
        negmax = sb("negmax", [P, NT])
        rowsum = sb("rowsum", [P, NT])
        rinv = sb("rinv", [P, NT])
        prob = sb("prob", [P, prob_off[NT]])
        pT_h = sb("pT_h", [P, prob_off[NT]], F32R)
        pT_l = sb("pT_l", [P, prob_off[NT]], F32R)
        res1 = sb("res1", [P, NT, C])
        stats = sb("stats", [P, NT, 6])
        mv = sb("mv", [P, NT, 2])
        veps = sb("veps", [P, NT])
        lrstd = sb("lrstd", [P, NT])
        nmr = sb("nmr", [P, NT])
        x1cur = sb("x1cur", [P, NT, C])
        x1_all = x_tok[:, :, 0:C]
        x1T_h = sb("x1T_h", [P, SEQ], F32R)
        x1T_l = sb("x1T_l", [P, SEQ], F32R)
        x1Ta_h, x1Ta_l = xT_h, xT_l
        gw = sb("gw", [P, E])
        gw_h = sb("gw_h", [P, E], F32R)
        gw_l = sb("gw_l", [P, E], F32R)
        logit = sb("logit", [P, NT, 2 * E])
        top8 = sb("top8", [P, NT, 8])
        pick = sb("pick", [P, NT, 8])
        marked = sb("marked", [P, NT, 2 * E])
        chosen = sb("chosen", [P, NT, E])
        lsum = sb("lsum", [P, NT])
        lmid = sb("lmid", [P, NT, E])
        ltanh = sb("ltanh", [P, NT, E])
        wsig = sb("wsig", [P, NT, E])
        wfull = sb("wfull", [P, NT, E])
        wpad = sb("wpad", [P, NT, P])
        wround = sb("wround", [P, NT, E], F32R)
        wT = sb("wT", [KW, NTOK], F32R)
        sel = sb("sel", [KW, E * F], F32R)
        Wg_raw = sb("Wg_raw", [P, FT])
        Wu_raw = sb("Wu_raw", [P, FT])
        Wd_raw = sb("Wd_raw", [P, NCH, C])
        Wg_h = sb("Wg_h", [P, FT], F32R)
        Wg_l = sb("Wg_l", [P, FT], F32R)
        Wu_h = sb("Wu_h", [P, FT], F32R)
        Wu_l = sb("Wu_l", [P, FT], F32R)
        Wd_h = sb("Wd_h", [P, NCH, C], F32R)
        Wd_l = sb("Wd_l", [P, NCH, C], F32R)
        silu = [Wg_raw[:, 0:SEQ], Wg_raw[:, SEQ:2 * SEQ]]
        su = [Wg_raw[:, 2 * SEQ:3 * SEQ], Wu_raw[:, 0:SEQ]]
        hid = [Wu_raw[:, SEQ:2 * SEQ], Wu_raw[:, 2 * SEQ:3 * SEQ]]
        wd_flat = Wd_raw[:].rearrange("p k c -> p (k c)")
        y_sb = wd_flat[:, 0:SEQ]
        r2 = wd_flat[:, SEQ:2 * SEQ].rearrange("p (i c) -> p i c", c=C)
        o_tok = wd_flat[:, 2 * SEQ:3 * SEQ].rearrange("p (i c) -> p i c", c=C)
        hT_h = [sb("hT_h0", [P, SEQ], F32R), sb("hT_h1", [P, SEQ], F32R)]
        hT_l = [sb("hT_l0", [P, SEQ], F32R), sb("hT_l1", [P, SEQ], F32R)]
        stats2 = sb("stats2", [P, NT, 6])
        mv2 = sb("mv2", [P, NT, 2])
        veps2 = sb("veps2", [P, NT])
        lrstd2 = sb("lrstd2", [P, NT])
        ident = sb("ident", [P, P])
        ident_r = sb("ident_r", [P, P], F32R)
        mask_f = sb("mask_f", [P, P])
        mask_r = sb("mask_r", [P, P], F32R)
        ones = sb("ones", [P, P])
        nhalf = sb("nhalf", [P, NT])

        x_in = [sem(f"x_in{b}") for b in range(NB)]
        wa_in, lora_in, wp_in, bn_in, gw_in = map(sem, ("wa_in", "lora_in", "wp_in", "bn_in", "gw_in"))
        wg_in, wu_in, wd_in = map(sem, ("wg_in", "wu_in", "wd_in"))
        x1_kept, out_stored = map(sem, ("x1_kept", "out_stored"))
        pool_const = sem("pool_const")
        dve_const = sem("dve_const")
        names = ("loraAT_pe loraAT_sb lora_pe wm_sb xT_pe xTh_sb xTl_sb wmT_pe wmT_sb wmpT_pe wmpT_sb gram_pe gram_sb "
                 "w2_pe w2_sb gw_pe wgw_sb moments_pe bn_var bn_rstd bn_ready w2s_sb wvo_pe wvoh_sb wvol_sb bias_pe "
                 "bias_sb tvb_sb wqkh_sb wqkl_sb gwh_sb gwl_sb").split()
        ss = {n: sem(n) for n in names}
        dve_step = sem("dve_step")
        names = ("rinv_sb nmr_sb q_pe q_sb qh_sb ql_sb k_pe k_sb kh_sb kl_sb v_pe vh_sb vl_sb score_pe max_sb prob_sb pT_pe pTh_sb "
                 "pTl_sb y_pe xres_sb res_free lnvar_sb lnrstd_sb x1_sb x1T_pe x1Th_sb x1Tl_sb logit_pe logit_sb "
                 "lmid_sb ltanh_sb wpad_sb wT_pe wT_sb").split()
        sa = {n: sem(n) for n in names}
        names = ("wsplit_h wsplit_l gate_pe gate_free up_pe up_free w_pe w_free silu_sb su_sb hid_sb hTh_sb hTl_sb "
                 "down_pe y_done y_sbd yT_pe r2_sb ln2var_sb ln2rstd_sb o_sb").split()
        sf = {n: sem(n) for n in names}

        block = ctx.enter_context(nc.Block())

        CONST_ONES, CONST_PAD, CONST_IDENT, CONST_MASK, CONST_FILL, CONST_SEL = 1, 2, 4, 5, 6, 13

        PRIMED = 1

        def blk(i):
            return slice(i * P, (i + 1) * P)

        @block.sync
        def _(sp):
            sp.wait_ge(pool_const, CONST_ONES)
            for b in range(NB):
                sp.dma_start(x_tok[:, b * NT:(b + 1) * NT, 0:C], xv[b]).then_inc(x_in[b], 16)
            sp.dma_start(Wm[:].rearrange("c j k -> c (j k)"),
                         W_attn.rearrange("(c j) k -> c (j k)", j=NJ)).then_inc(wa_in, 16)
            sp.dma_start(Wp[:], W_proj).then_inc(wp_in, 16)
            sp.dma_start(bn_rows[0:NJ, :], bn_gamma.rearrange("(j d) -> j d", d=C)).then_inc(bn_in, 16)
            sp.dma_start(bn_rows[NJ:2 * NJ, :], bn_beta.rearrange("(j d) -> j d", d=C)).then_inc(bn_in, 16)
            sp.dma_start(gw[:], gate_w).then_inc(gw_in, 16)
            sp.wait_ge(pool_const, CONST_PAD)
            for raw, shared, routed, done in ((Wg_raw, sh_gate, exp_gate, wg_in), (Wu_raw, sh_up, exp_up, wu_in)):
                sp.dma_start(raw[:, 0:SHF].rearrange("c (s f) -> c s f", s=S),
                             shared.rearrange("s c f -> c s f")).then_inc(done, 16)
                sp.dma_start(raw[:, NSH * P:FT].rearrange("c (e f) -> c e f", e=E),
                             routed.rearrange("e c f -> c e f")).then_inc(done, 16)
            shd = sh_down.rearrange("s f c -> (s f) c")
            sp.dma_start(Wd_raw[:, 0:NSH - 1, :],
                         shd[0:(NSH - 1) * P].rearrange("(k p) c -> p k c", p=P)).then_inc(wd_in, 16)
            sp.dma_start(Wd_raw[0:SH_TAIL, NSH - 1, :], shd[(NSH - 1) * P:SHF]).then_inc(wd_in, 16)
            sp.dma_start(Wd_raw[:, NSH:NCH, :],
                         exp_down.rearrange("e f c -> (e f) c").rearrange("(k p) c -> p k c", p=P)).then_inc(wd_in, 16)

            def keep_x1(b):
                need(sp, x1_kept, 48 * b, PRIMED)
                sp.wait_ge(sa["x1_sb"], b + 1)
                sp.dma_start(x1_all[:, bass.ds(b * NT, NT), :], x1cur[:]).then_inc(x1_kept, 16)
                sp.wait_ge(sa["x1Tl_sb"], b + 1)
                sp.dma_start(x1Ta_h[:, bass.ds(b * SEQ, SEQ)].bitcast(F32), x1T_h[:].bitcast(F32)).then_inc(x1_kept, 16)
                sp.dma_start(x1Ta_l[:, bass.ds(b * SEQ, SEQ)].bitcast(F32), x1T_l[:].bitcast(F32)).then_inc(x1_kept, 16)

            def store(g):
                need(sp, out_stored, 16 * g, PRIMED)
                sp.wait_ge(sf["o_sb"], g + 1)
                sp.dma_start(ov[g], o_tok[:]).then_inc(out_stored, 16)

            for b in range(NB):
                keep_x1(b)
            for g in range(NB):
                store(g)
            sp.wait_ge(out_stored, 16 * NB + PRIMED)

        @block.gpsimd
        def _(pool):
            made = [0]

            def const(ins):
                made[0] += 1
                ins.then_inc(pool_const, 1)
                pool.wait_ge(pool_const, made[0])

            g = nc.gpsimd
            const(g.memset(x_tok[:, :, C:C + 2], 1.0))
            g.memset(Wg_raw[:, SHF:NSH * P], 0.0)
            g.memset(Wu_raw[:, SHF:NSH * P], 0.0)
            const(g.memset(Wd_raw[:, NSH - 1, :], 0.0))
            g.memset(ones[:], 1.0).then_inc(x1_kept, PRIMED)
            g.memset(nhalf[:], -0.5).then_inc(out_stored, PRIMED)
            const(g.memset(mask_f[:], 0.0))
            const(g.affine_select(out=ident[:], in_=ones[:], compare_op=ALU.is_equal, fill=0.0, base=0,
                                  pattern=[[-1, P]], channel_multiplier=1))
            const(g.affine_select(out=mask_f[:], in_=mask_f[:], compare_op=ALU.is_ge, fill=MASKED, base=0,
                                  pattern=[[-1, P]], channel_multiplier=1))
            g.memset(logit[:], BIG)
            g.memset(pick[:], BIG)
            const(g.memset(wpad[:], 0.0))
            const(g.memset(sel[:].bitcast(F32), 0.0))
            for row in (0, LO_ROW):
                part = sel[row:row + E, :]
                const(g.memset(part.bitcast(F32), 1.0))
                const(g.affine_select(out=part, in_=part.bitcast(F32), compare_op=ALU.is_ge, fill=0.0, base=0,
                                      pattern=[[1, E * F]], channel_multiplier=-F))
                const(g.affine_select(out=part, in_=part.bitcast(F32), compare_op=ALU.is_ge, fill=0.0, base=F - 1,
                                      pattern=[[-1, E * F]], channel_multiplier=F))
            assert made[0] == CONST_SEL
            pool.wait_ge(ss["bn_var"], 1)
            nc.gpsimd.tensor_tensor(out=rstd[:], in0=var[:], in1=nhalf[:, 0:NJ], op=ALU.pow).then_inc(ss["bn_rstd"], 1)

            def split_q(b):
                pool.wait_ge(sa["qh_sb"], b + 1)
                nc.gpsimd.tensor_tensor(out=q_l[:], in0=q_all[:, bass.ds(b * SEQ, SEQ)], in1=q_h[:].bitcast(F32),
                                        op=ALU.subtract).then_inc(sa["ql_sb"], 1)

            def split_k(b):
                cols = slice(b * SEQ, (b + 1) * SEQ)
                pool.wait_ge(sa["kh_sb"], b + 1)
                nc.gpsimd.tensor_tensor(out=k_l[:, cols], in0=kf[:], in1=k_h[:, cols].bitcast(F32),
                                        op=ALU.subtract).then_inc(sa["kl_sb"], 1)

            def residual_base(b):
                need(pool, sa["res_free"], b)
                nc.gpsimd.tensor_tensor(out=x_res[:], in0=x_tok[:, bass.ds(b * NT, NT), 0:C],
                                        in1=bias_tok[:].unsqueeze(1).broadcast_to((P, NT, C)),
                                        op=ALU.add).then_inc(sa["xres_sb"], 1)

            def ln_rstd(b):
                pool.wait_ge(sa["lnvar_sb"], b + 1)
                nc.gpsimd.tensor_tensor(out=lrstd[:], in0=veps[:], in1=nhalf[:], op=ALU.pow).then_inc(sa["lnrstd_sb"], 1)

            def split_weight(n, raw, hi, lo):
                pool.wait_ge(sf["wsplit_h"], n + 1)
                nc.gpsimd.tensor_tensor(out=lo, in0=raw, in1=hi.bitcast(F32), op=ALU.subtract).then_inc(sf["wsplit_l"], 1)

            def split_hidden(g, j):
                n = g * NCH + j
                pool.wait_ge(sf["hTh_sb"], n + 1)
                nc.gpsimd.tensor_tensor(out=hT_l[j % 2][:], in0=hid[j % 2], in1=hT_h[j % 2][:].bitcast(F32),
                                        op=ALU.subtract).then_inc(sf["hTl_sb"], 1)

            def ln2_rstd(g):
                pool.wait_ge(sf["ln2var_sb"], g + 1)
                nc.gpsimd.tensor_tensor(out=lrstd2[:], in0=veps2[:], in1=nhalf[:], op=ALU.pow).then_inc(sf["ln2rstd_sb"], 1)

            nc.gpsimd.memset(q_all[:, NTOK:NTOK + SEQ], 0.0).then_inc(sa["wT_sb"], PRIMED)
            split_k(0)
            pool.wait_ge(ss["bias_sb"], 1)
            residual_base(0)
            split_k(1)
            split_q(1)
            split_k(2)
            split_k(3)
            split_q(2)
            split_weight(2, Wd_raw[:], Wd_h[:], Wd_l[:])
            with pool.Fori(1, NB - 1) as b:
                ln_rstd(b - 1)
                residual_base(b)
                split_q(b + 2)
            ln_rstd(NB - 2)
            residual_base(NB - 1)
            split_hidden(0, 0)
            ln_rstd(NB - 1)

            for j in range(1, NCH):
                split_hidden(0, j)
            with pool.Fori(1, NB) as g:
                for j in range(NCH):
                    split_hidden(g, j)
                    if j == 7:
                        ln2_rstd(g - 1)
            ln2_rstd(NB - 1)

        @block.tensor
        def _(pe):
            def mm3(dst, lh, ll, rh, rl, start=True, stop=True, skip=False):
                nc.tensor.matmul(dst, lh, rh, start=start, stop=False, skip_group_check=skip)
                nc.tensor.matmul(dst, lh, rl, start=False, stop=False, skip_group_check=skip)
                return nc.tensor.matmul(dst, ll, rh, start=False, stop=stop, skip_group_check=skip)

            def gram_of(b):
                pe.wait_ge(x_in[b], 16)
                for t in range(b * NT, (b + 1) * NT):
                    last = nc.tensor.matmul(bank[3][:, 0:C + 1], x_tok[:, t, 0:C], x_tok[:, t, 0:C + 1],
                                            start=(t == 0), stop=(t == NB * NT - 1))
                if b == NB - 1:
                    last.then_inc(ss["gram_pe"], 1)

            def transpose_x(b):
                for i in range(NT):
                    last = nc.tensor.transpose(bank[4 + b][:, blk(i)], x_tok[:, b * NT + i, 0:C], ident[:])
                last.then_inc(ss["xT_pe"], 1)

            gram_of(0)
            pe.wait_ge(pool_const, CONST_IDENT)
            pe.wait_ge(lora_in, 64)
            nc.tensor.transpose(bank[0][0:R, 0:P], loA[:], ident[:])
            nc.tensor.transpose(bank[0][0:R, P:2 * P], pA[:], ident[:]).then_inc(ss["loraAT_pe"], 1)
            gram_of(1)
            pe.wait_ge(ss["loraAT_sb"], 1)
            nc.tensor.matmul(bank[1][:, 0:D3], loAT[:], loB[:], start=True, stop=True).then_inc(ss["lora_pe"], 1)
            nc.tensor.matmul(bank[2][:, 0:C], pAT[:], pB[:], start=True, stop=True).then_inc(ss["lora_pe"], 1)
            gram_of(2)
            pe.wait_ge(ss["wm_sb"], 2)
            for j in range(NJ):
                last = nc.tensor.transpose(bank[0][:, blk(j)], Wm[:, j, :], ident[:])
            last.then_inc(ss["wmT_pe"], 1)
            nc.tensor.transpose(bank[2][:, 0:C], Wmp[:], ident[:]).then_inc(ss["wmpT_pe"], 1)
            gram_of(3)
            transpose_x(0)
            pe.wait_ge(ss["wmpT_sb"], 1)
            nc.tensor.matmul(bank[2][:, P:2 * P], Wp[:], WmpT[:], start=True, stop=True).then_inc(ss["w2_pe"], 1)
            pe.wait_ge(ss["gram_sb"], 1)
            pe.wait_ge(ss["wmT_sb"], 1)
            nc.tensor.matmul(bank[1][:, 0:D3], gram[:, 0:C], WmT[:], start=True, stop=True).then_inc(ss["gw_pe"], 1)
            nc.tensor.transpose(bank[0][:, 0:C], WmT[:, 2 * C:3 * C], ident[:])
            pe.wait_ge(bn_in, 32)
            nc.tensor.transpose(bank[0][:, P:P + 2 * NJ], bn_rows[:], ident[0:2 * NJ, 0:2 * NJ])
            transpose_x(1)
            pe.wait_ge(ss["wgw_sb"], 1)
            for j in range(NJ):
                nc.tensor.matmul(bank[0][:, 160 + j:161 + j], wgw[:, blk(j)], ones[:, 0:1], start=True, stop=True)
                last = nc.tensor.matmul(bank[0][:, 176 + j:177 + j], WmT[:, blk(j)], gram[:, C:C + 1],
                                        start=True, stop=True)
            last.then_inc(ss["moments_pe"], 1)
            transpose_x(2)
            transpose_x(3)

            def project_q(b):
                need(pe, sa["q_sb"], b)
                cols = slice(b * SEQ, (b + 1) * SEQ)
                mm3(ps_q[:], WqkT_h[:, blk(0)], WqkT_l[:, blk(0)], xT_h[:, cols], xT_l[:, cols]).then_inc(sa["q_pe"], 1)

            def project_k(b):
                need(pe, sa["k_sb"], b)
                cols = slice(b * SEQ, (b + 1) * SEQ)
                mm3(ps_k[:], WqkT_h[:, blk(1)], WqkT_l[:, blk(1)], xT_h[:, cols], xT_l[:, cols]).then_inc(sa["k_pe"], 1)

            def project_v(b):
                need(pe, sa["vl_sb"], b)
                for i in range(NT):
                    t = b * NT + i
                    last = mm3(ps_v[:, blk(i)], xT_h[:, blk(t)], xT_l[:, blk(t)], WvoT_h[:], WvoT_l[:])
                last.then_inc(sa["v_pe"], 1)

            def scores(b):
                pe.wait_ge(sa["ql_sb"], b + 1)
                need(pe, sa["prob_sb"], NT * b)
                for i in range(NT):
                    w = (i + 1) * P
                    n, at = score_at[i]
                    dst = ps_score[n]
                    mm3(dst[:, at:at + w], q_h[:, blk(i)], q_l[:, blk(i)], k_h[:, bass.ds(b * SEQ, w)],
                        k_l[:, bass.ds(b * SEQ, w)], stop=False)
                    nc.tensor.matmul(dst[:, at + i * P:at + w], ident_r[:], mask_r[:], start=False,
                                     stop=True).then_inc(sa["score_pe"], 1)

            def transpose_probs(b, first):
                for n, (i0, tiles) in enumerate(pT_parts):
                    pe.wait_ge(sa["prob_sb"], NT * b + i0 + tiles)
                    if first and n == 2:
                        pe.wait_ge(sa["q_sb"], NB)
                    o = prob_off[i0]
                    for c in range((prob_off[i0 + tiles] - o) // P):
                        last = nc.tensor.transpose(ps_pT[n][:, blk(c)], prob[:, o + c * P:o + (c + 1) * P], ident[:])
                    last.then_inc(sa["pT_pe"], 1)

            def attend(b, first, parts):
                if 0 not in parts:
                    pass
                elif first:
                    pe.wait_ge(sa["k_sb"], NB)
                else:
                    pe.wait_ge(sa["res_free"], b)
                for n in parts:
                    i0, tiles = pT_parts[n]
                    pe.wait_ge(sa["pTl_sb"], 3 * b + n + 1)
                    for i in range(i0, i0 + tiles):
                        for j in range(i + 1):
                            at = prob_off[i] + j * P
                            last = mm3(ps_y[:, blk(i)], pT_h[:, at:at + P], pT_l[:, at:at + P],
                                       v_h[:, bass.ds(b * NT + j, 1), :].rearrange("p a c -> p (a c)"),
                                       v_l[:, bass.ds(b * NT + j, 1), :].rearrange("p a c -> p (a c)"),
                                       start=(j == 0), stop=(j == i))
                if 2 in parts:
                    last.then_inc(sa["y_pe"], 1)

            def transpose_x1(b):
                need(pe, sa["wT_sb"], b, PRIMED)
                pe.wait_ge(sa["x1_sb"], b + 1)
                for i in range(NT):
                    last = nc.tensor.transpose(ps_x1[:, blk(i)], x1cur[:, i, :], ident[:])
                last.then_inc(sa["x1T_pe"], 1)

            def logits(b):
                pe.wait_ge(sa["x1Tl_sb"], b + 1)
                for i in range(NT):
                    last = mm3(ps_x1[:, i * E:(i + 1) * E], x1T_h[:, blk(i)], x1T_l[:, blk(i)], gw_h[:], gw_l[:])
                last.then_inc(sa["logit_pe"], 1)

            def transpose_w(b):
                pe.wait_ge(sa["wpad_sb"], b + 1)
                for i in range(NT):
                    last = nc.tensor.transpose(ps_x1[:, blk(i)], wpad[:, i, :], ident[:])
                last.then_inc(sa["wT_pe"], 1)

            pe.wait_ge(ss["xTl_sb"], 1)
            pe.wait_ge(ss["wqkl_sb"], 1)
            pe.wait_ge(ss["bn_var"], 1)
            project_q(0)
            project_k(0)
            pe.wait_ge(ss["w2s_sb"], 1)
            nc.tensor.matmul(bank[3][:, P:2 * P], Wv[:], W2s[:], start=True, stop=True).then_inc(ss["wvo_pe"], 1)
            pe.wait_ge(ss["tvb_sb"], 1)
            nc.tensor.matmul(bank[4][:, 0:C], tv_b[:], W2T[:], start=True, stop=True).then_inc(ss["bias_pe"], 1)

            pe.wait_ge(dve_const, 2)
            pe.wait_ge(ss["xTl_sb"], NB)
            pe.wait_ge(sa["kl_sb"], 1)
            scores(0)
            project_q(1)
            project_k(1)
            pe.wait_ge(ss["wvol_sb"], 1)
            pe.wait_ge(ss["w2_sb"], 1)
            project_v(0)
            project_v(1)
            for b in range(2, NB):
                project_q(b)
                project_k(b)
                project_v(b)

            def attention(b, first=False):
                transpose_probs(b, first)
                if first:
                    pe.wait_ge(sa["kl_sb"], NB)
                scores(b + 1)
                if not first:
                    transpose_x1(b - 1)
                if first:
                    pe.wait_ge(sa["vl_sb"], NB)
                attend(b, first, (0, 1))
                if not first:
                    logits(b - 1)
                attend(b, first, (2,))
                if not first:
                    transpose_w(b - 1)

            attention(0, first=True)
            pe.wait_ge(ss["gwl_sb"], 1)
            with pe.Fori(1, NB - 1) as b:
                attention(b)
            transpose_probs(NB - 1, False)

            def up_chunk(g, j):
                n = g * NCH + j
                if j == 0:
                    pe.wait_ge(x1_kept, 48 * g + 48 + PRIMED)
                xh, xl = x1Ta_h[:, bass.ds(g * SEQ, SEQ)], x1Ta_l[:, bass.ds(g * SEQ, SEQ)]
                need(pe, sf["silu_sb"], n - 1)
                mm3(ps_gate[j % 2][:], Wg_h[:, blk(j)], Wg_l[:, blk(j)], xh, xl).then_inc(sf["gate_pe"], 1)
                need(pe, sf["su_sb"], n - 1)
                if j >= NSH:
                    need(pe, sf["hid_sb"], g * NRT + max(0, j - NSH - 1))
                mm3(ps_up[j % 2][:], Wu_h[:, blk(j)], Wu_l[:, blk(j)], xh, xl).then_inc(sf["up_pe"], 1)
                if j == NSH:
                    pe.wait_ge(sa["wT_sb"], g + 1 + PRIMED)
                if j >= NSH:
                    c = j - NSH
                    nc.tensor.matmul(ps_w[j % 2][:], sel[:, blk(c)], wT[:, bass.ds(g * SEQ, SEQ)],
                                     start=True, stop=True).then_inc(sf["w_pe"], 1)

            def down_chunk(g, j):
                n = g * NCH + j
                if j == 0:
                    need(pe, sf["y_sbd"], g)
                pe.wait_ge(sf["hTl_sb"], n + 1)
                mm3(ps_down[:], Wd_h[:, j, :], Wd_l[:, j, :], hT_h[j % 2][:], hT_l[j % 2][:],
                    start=(j == 0), stop=(j == NCH - 1)).then_inc(sf["down_pe"], 1)

            def transpose_y(g):
                pe.wait_ge(sf["y_sbd"], g + 1)
                for i in range(NT):
                    last = nc.tensor.transpose(ps_out[:, blk(i)], y_sb[:, blk(i)], ident[:])
                last.then_inc(sf["yT_pe"], 1)

            def group(g, first=False):
                for j in range(NCH):
                    up_chunk(g, j)
                    if j >= 2:
                        down_chunk(g, j - 2)
                    elif not first:
                        down_chunk(g - 1, NCH - 2 + j)
                    if j == 3 and not first:
                        transpose_y(g - 1)
                    if first:
                        if j == 0:
                            attend(NB - 1, False, (0, 1))
                            transpose_x1(NB - 2)
                        if j == 1:
                            attend(NB - 1, False, (2,))
                            logits(NB - 2)
                            pe.wait_ge(sa["res_free"], NB)
                            pe.wait_ge(sf["wsplit_l"], 3)
                        if j == 3:
                            transpose_w(NB - 2)
                        if j == 5:
                            transpose_x1(NB - 1)
                        if j == 7:
                            logits(NB - 1)
                        if j == 10:
                            transpose_w(NB - 1)

            pe.wait_ge(sf["wsplit_l"], 2)
            pe.wait_ge(pool_const, CONST_SEL)
            group(0, first=True)
            pe.wait_ge(sa["wT_sb"], NB + PRIMED)
            with pe.Fori(1, NB) as g:
                group(g)
            down_chunk(NB - 1, NCH - 2)
            down_chunk(NB - 1, NCH - 1)
            transpose_y(NB - 1)

        @block.scalar
        def _(act):
            act.dma_start(loA[:], attn_A).then_inc(lora_in, 16)
            act.dma_start(pA[:], proj_A).then_inc(lora_in, 16)
            act.dma_start(loB[:], attn_B).then_inc(lora_in, 16)
            act.dma_start(pB[:], proj_B).then_inc(lora_in, 16)
            act.preload_act_table(ACT.Exp)

            act.wait_ge(ss["loraAT_pe"], 1)
            nc.scalar.activation(loAT[:], bank[0][0:R, 0:P], ACT.Copy)
            nc.scalar.activation(pAT[:], bank[0][0:R, P:2 * P], ACT.Copy).then_inc(ss["loraAT_sb"], 1)
            def xT_high(b):
                act.wait_ge(ss["xT_pe"], b + 1)
                nc.scalar.activation(xT_h[:, b * SEQ:(b + 1) * SEQ], bank[4 + b][:], ACT.Copy).then_inc(ss["xTh_sb"], 1)

            act.wait_ge(ss["wmT_pe"], 1)
            nc.scalar.activation(WmT[:].rearrange("p (c j) -> p j c", j=NJ),
                                 bank[0][:, 0:D3].rearrange("p (j c) -> p j c", j=NJ), ACT.Copy).then_inc(ss["wmT_sb"], 1)
            act.wait_ge(ss["wmpT_pe"], 1)
            nc.scalar.activation(WmpT[:], bank[2][:, 0:C], ACT.Copy).then_inc(ss["wmpT_sb"], 1)
            act.wait_ge(ss["gram_pe"], 1)
            nc.scalar.activation(gram[:, 0:C + 1], bank[3][:, 0:C + 1], ACT.Copy).then_inc(ss["gram_sb"], 1)
            xT_high(0)
            act.wait_ge(ss["w2_pe"], 1)
            nc.scalar.activation(W2T[:], bank[2][:, P:2 * P], ACT.Copy).then_inc(ss["w2_sb"], 1)
            act.wait_ge(ss["wmT_sb"], 1)
            nc.scalar.activation(WqkT_h[:], WmT[:, 0:2 * C], ACT.Copy).then_inc(ss["wqkh_sb"], 1)

            def affine_q(b):
                act.wait_ge(sa["q_pe"], b + 1)
                nc.scalar.activation(q_all[:, b * SEQ:(b + 1) * SEQ], ps_q[:], ACT.Identity, bias=qk_t[:, 0:1],
                                     scale=qk_s[:, 0:1]).then_inc(sa["q_sb"], 1)

            def affine_k(b):
                act.wait_ge(sa["k_pe"], b + 1)
                need(act, sa["kl_sb"], b)
                nc.scalar.activation(kf[:], ps_k[:], ACT.Identity, bias=qk_t[:, 1:2],
                                     scale=qk_s[:, 1:2]).then_inc(sa["k_sb"], 1)

            def value_high(b):
                act.wait_ge(sa["v_pe"], b + 1)
                nc.scalar.activation(v_h[:, b * NT:(b + 1) * NT, :].rearrange("p i c -> p (i c)"), ps_v[:],
                                     ACT.Copy).then_inc(sa["vh_sb"], 1)

            def probs(b, tiles):
                if 0 in tiles:
                    need(act, sa["rinv_sb"], b)
                for i in tiles:
                    act.wait_ge(sa["max_sb"], NT * b + max(2, i + 1))
                    n, at = score_at[i]
                    nc.scalar.activation(prob[:, prob_off[i]:prob_off[i + 1]], ps_score[n][:, at:at + (i + 1) * P],
                                         ACT.Exp, bias=negmax[:, i:i + 1],
                                         accum_out=rowsum[:, i:i + 1]).then_inc(sa["prob_sb"], 1)

            def q_high(b):
                nc.scalar.activation(q_h[:], q_all[:, bass.ds(b * SEQ, SEQ)], ACT.Copy).then_inc(sa["qh_sb"], 1)

            def probsT_high(b, n):
                act.wait_ge(sa["pT_pe"], 3 * b + n + 1)
                i0, tiles = pT_parts[n]
                lo, hi = prob_off[i0], prob_off[i0 + tiles]
                nc.scalar.activation(pT_h[:, lo:hi], ps_pT[n][:, 0:hi - lo], ACT.Copy).then_inc(sa["pTh_sb"], 1)

            def normalise(b):
                need(act, x1_kept, 48 * b, PRIMED)
                act.wait_ge(sa["nmr_sb"], b + 1)
                for i in range(NT):
                    ins = nc.scalar.activation(x1cur[:, i, :], res1[:, i, :], ACT.Identity, bias=nmr[:, i:i + 1],
                                               scale=lrstd[:, i:i + 1])
                ins.then_inc(sa["x1_sb"], 1)

            def x1T_high(b):
                act.wait_ge(sa["x1T_pe"], b + 1)
                nc.scalar.activation(x1T_h[:], ps_x1[:], ACT.Copy).then_inc(sa["x1Th_sb"], 1)

            def router_tanh(b):
                act.wait_ge(sa["lmid_sb"], b + 1)
                nc.scalar.activation(ltanh[:], lmid[:], ACT.Tanh).then_inc(sa["ltanh_sb"], 1)

            def weight_high(n, raw, hi, arrived, count):
                act.wait_ge(arrived, count)
                nc.scalar.activation(hi, raw, ACT.Copy).then_inc(sf["wsplit_h"], 1)

            for b in range(1, NB):
                xT_high(b)
            weight_high(0, Wg_raw[:], Wg_h[:], wg_in, 32)
            act.wait_ge(ss["bn_ready"], 1)
            affine_q(0)
            affine_k(0)
            act.wait_ge(ss["wvo_pe"], 1)
            nc.scalar.activation(WvoT_h[:], bank[3][:, P:2 * P], ACT.Copy).then_inc(ss["wvoh_sb"], 1)
            act.wait_ge(ss["bias_pe"], 1)
            nc.scalar.activation(bias_tok[:], bank[4][:, 0:C], ACT.Copy).then_inc(ss["bias_sb"], 1)
            probs(0, range(NT))
            affine_q(1)
            act.wait_ge(sa["q_sb"], 2)
            q_high(1)
            affine_k(1)
            value_high(0)
            value_high(1)
            weight_high(1, Wu_raw[:], Wu_h[:], wu_in, 32)
            for b in range(2, NB):
                affine_q(b)
                affine_k(b)
                value_high(b)

            def attention(b, first=False):
                for n in range(3):
                    probsT_high(b, n)
                if not first:
                    normalise(b - 1)
                probs(b + 1, (0, 1))
                if not first:
                    x1T_high(b - 1)
                probs(b + 1, (2, 3))
                if first:
                    act.wait_ge(sa["q_sb"], NB)
                q_high(b + 2)
                if not first:
                    router_tanh(b - 1)

            attention(0, first=True)
            weight_high(2, Wd_raw[:], Wd_h[:], wd_in, 48)
            with act.Fori(1, NB - 1) as b:
                attention(b)
            act.preload_act_table(ACT.Silu)
            for n in range(3):
                probsT_high(NB - 1, n)

            def gate_silu(g, j):
                n = g * NCH + j
                act.wait_ge(sf["gate_pe"], n + 1)
                need(act, sf["su_sb"], n - 1)
                nc.scalar.activation(silu[j % 2], ps_gate[j % 2][:], ACT.Silu).then_inc(sf["silu_sb"], 1)

            def hidden_high(g, j):
                n = g * NCH + j
                if j < NSH:
                    act.wait_ge(sf["su_sb"], n + 1)
                else:
                    act.wait_ge(sf["hid_sb"], g * NRT + j - NSH + 1)
                need(act, sf["down_pe"], n - 1)
                nc.scalar.activation(hT_h[j % 2][:], hid[j % 2], ACT.Copy).then_inc(sf["hTh_sb"], 1)

            def down_out(g):
                act.wait_ge(sf["down_pe"], (g + 1) * NCH)
                nc.scalar.activation(y_sb, ps_down[:], ACT.Copy).then_inc(sf["y_sbd"], 1)

            def group(g, first=False):
                for j in range(NCH):
                    gate_silu(g, j)
                    if j >= 1:
                        hidden_high(g, j - 1)
                    elif not first:
                        hidden_high(g - 1, NCH - 1)
                    if j == 2 and not first:
                        down_out(g - 1)
                    if first:
                        if j == 0:
                            normalise(NB - 2)
                            x1T_high(NB - 2)
                        if j == 3:
                            router_tanh(NB - 2)
                        if j == 4:
                            normalise(NB - 1)
                        if j == 6:
                            x1T_high(NB - 1)
                        if j == 9:
                            router_tanh(NB - 1)

            act.wait_ge(sf["wsplit_l"], 2)
            group(0, first=True)
            with act.Fori(1, NB) as g:
                group(g)
            hidden_high(NB - 1, NCH - 1)
            down_out(NB - 1)

        @block.vector
        def _(dve):
            v = nc.vector
            st = Steps(dve, dve_step)
            dve.wait_ge(pool_const, CONST_MASK)
            v.tensor_copy(ident_r[:], ident[:]).then_inc(dve_const, 1)
            v.tensor_copy(mask_r[:], mask_f[:]).then_inc(dve_const, 1)
            dve.wait_ge(ss["lora_pe"], 1)
            dve.wait_ge(wa_in, 16)
            wm_flat = Wm[:].rearrange("c j k -> c (j k)")
            v.tensor_tensor(wm_flat, bank[1][:, 0:D3], wm_flat, ALU.add).then_inc(ss["wm_sb"], 1)
            dve.wait_ge(ss["lora_pe"], 2)
            dve.wait_ge(wp_in, 16)
            v.tensor_tensor(Wmp[:], bank[2][:, 0:C], Wp[:], ALU.add).then_inc(ss["wm_sb"], 1)
            def xT_low(b):
                dve.wait_ge(ss["xTh_sb"], b + 1)
                cols = slice(b * SEQ, (b + 1) * SEQ)
                v.tensor_tensor(xT_l[:, cols], bank[4 + b][:], xT_h[:, cols].bitcast(F32),
                                ALU.subtract).then_inc(ss["xTl_sb"], 1)

            def weight_low(n, raw, hi, lo):
                dve.wait_ge(sf["wsplit_h"], n + 1)
                v.tensor_tensor(lo, raw, hi.bitcast(F32), ALU.subtract).then_inc(sf["wsplit_l"], 1)

            dve.wait_ge(ss["gw_pe"], 1)
            v.tensor_tensor(wgw[:], bank[1][:, 0:D3], WmT[:], ALU.mult).then_inc(ss["wgw_sb"], 1)
            dve.wait_ge(ss["wqkh_sb"], 1)
            v.tensor_tensor(WqkT_l[:], WmT[:, 0:2 * C], WqkT_h[:].bitcast(F32), ALU.subtract).then_inc(ss["wqkl_sb"], 1)
            xT_low(0)
            xT_low(1)
            dve.wait_ge(gw_in, 16)
            v.tensor_copy(gw_h[:], gw[:]).then_inc(ss["gwh_sb"], 1)
            dve.wait_ge(ss["moments_pe"], 1)
            st.done(v.tensor_copy(bn_cols[:], bank[0][:, P:P + 2 * NJ]))
            st.done(v.tensor_copy(Wv[:], bank[0][:, 0:C]))
            st.done(v.tensor_scalar(mean[:], bank[0][:, 176:176 + NJ], 1.0 / NTOK, None, ALU.mult))
            st.wait()
            st.done(v.tensor_tensor(msq[:], mean[:], mean[:], ALU.mult))
            st.wait()
            st.done(v.scalar_tensor_tensor(out=var[:], in0=bank[0][:, 160:160 + NJ], scalar=1.0 / NTOK, in1=msq[:],
                                           op0=ALU.mult, op1=ALU.subtract))
            st.wait()
            v.tensor_scalar(var[:], var[:], 0.0, EPS, ALU.max, ALU.add).then_inc(ss["bn_var"], 1)
            dve.wait_ge(ss["gwh_sb"], 1)
            v.tensor_tensor(gw_l[:], gw[:], gw_h[:].bitcast(F32), ALU.subtract).then_inc(ss["gwl_sb"], 1)
            xT_low(2)
            xT_low(3)
            dve.wait_ge(ss["bn_rstd"], 1)
            st.done(v.tensor_tensor(bn_s[:], rstd[:], bn_cols[:, 0:NJ], ALU.mult))
            st.wait()
            st.done(v.tensor_tensor(mst[:], mean[:], bn_s[:], ALU.mult))
            st.wait()
            st.done(v.tensor_tensor(bn_t[:], bn_cols[:, NJ:2 * NJ], mst[:], ALU.subtract))
            st.wait()
            v.tensor_scalar(qk_s[:, 0:1], bn_s[:, 0:1], SCALE, None, ALU.mult)
            v.tensor_copy(qk_s[:, 1:2], bn_s[:, 1:2])
            v.tensor_scalar(qk_t[:, 0:1], bn_t[:, 0:1], SCALE, None, ALU.mult)
            v.tensor_copy(qk_t[:, 1:2], bn_t[:, 1:2]).then_inc(ss["bn_ready"], 1)
            dve.wait_ge(ss["w2_sb"], 1)
            v.tensor_scalar(W2s[:], W2T[:], bn_s[:, 2:3], None, ALU.mult).then_inc(ss["w2s_sb"], 1)
            v.tensor_scalar(tv_b[:], ones[:], bn_t[:, 2:3], None, ALU.mult).then_inc(ss["tvb_sb"], 1)

            def k_high(b):
                dve.wait_ge(sa["k_sb"], b + 1)
                v.tensor_copy(k_h[:, b * SEQ:(b + 1) * SEQ], kf[:]).then_inc(sa["kh_sb"], 1)

            def value_low(b):
                dve.wait_ge(sa["vh_sb"], b + 1)
                tiles = slice(b * NT, (b + 1) * NT)
                v.tensor_tensor(v_l[:, tiles, :].rearrange("p i c -> p (i c)"), ps_v[:],
                                v_h[:, tiles, :].rearrange("p i c -> p (i c)").bitcast(F32),
                                ALU.subtract).then_inc(sa["vl_sb"], 1)

            def row_max(b):
                for i in range(NT):
                    dve.wait_ge(sa["score_pe"], NT * b + max(2, i + 1))
                    n, at = score_at[i]
                    v.tensor_reduce(negmax[:, i:i + 1], ps_score[n][:, at:at + (i + 1) * P], AX.X, ALU.max,
                                    negate=True).then_inc(sa["max_sb"], 1)

            def probsT_low(b, n):
                dve.wait_ge(sa["pTh_sb"], 3 * b + n + 1)
                i0, tiles = pT_parts[n]
                lo, hi = prob_off[i0], prob_off[i0 + tiles]
                v.tensor_tensor(pT_l[:, lo:hi], ps_pT[n][:, 0:hi - lo], pT_h[:, lo:hi].bitcast(F32),
                                ALU.subtract).then_inc(sa["pTl_sb"], 1)

            def row_stats(steps, src, st6, mean_var, var_eps, var_ready):
                for i in range(NT):
                    v.bn_stats(st6[:, i, :], src[:, i, :])
                dve.drain()
                for i in range(NT):
                    steps.done(v.bn_aggr(mean_var[:, i, :], st6[:, i, :]))
                steps.wait()
                v.tensor_scalar(var_eps[:], mean_var[:, :, 1], EPS, None, ALU.add).then_inc(var_ready, 1)

            def sum_inverse(b):
                dve.wait_ge(sa["prob_sb"], NT * b + NT)
                v.reciprocal(rinv[:], rowsum[:]).then_inc(sa["rinv_sb"], 1)

            def residual(b, steps):
                dve.wait_ge(sa["rinv_sb"], b + 1)
                need(dve, sa["x1_sb"], b)
                dve.wait_ge(sa["xres_sb"], b + 1)
                dve.wait_ge(sa["y_pe"], b + 1)
                for i in range(NT):
                    ins = v.scalar_tensor_tensor(out=res1[:, i, :], in0=ps_y[:, blk(i)], scalar=rinv[:, i:i + 1],
                                                 in1=x_res[:, i, :], op0=ALU.mult, op1=ALU.add)
                ins.then_inc(sa["res_free"], 1)
                dve.wait_ge(sa["res_free"], b + 1)
                row_stats(steps, res1, stats, mv, veps, sa["lnvar_sb"])

            def norm_bias(b):
                dve.wait_ge(sa["lnrstd_sb"], b + 1)
                v.scalar_tensor_tensor(out=nmr[:], in0=mv[:, :, 0], scalar=-1.0, in1=lrstd[:], op0=ALU.mult,
                                       op1=ALU.mult).then_inc(sa["nmr_sb"], 1)

            def x1T_low(b):
                dve.wait_ge(sa["x1Th_sb"], b + 1)
                v.tensor_tensor(x1T_l[:], ps_x1[:], x1T_h[:].bitcast(F32), ALU.subtract).then_inc(sa["x1Tl_sb"], 1)

            def route_top2(b, steps):
                dve.wait_ge(sa["logit_pe"], b + 1)
                v.tensor_copy(logit[:, :, 0:E], ps_x1[:, 0:NT * E].rearrange("p (i e) -> p i e",
                                                                             e=E)).then_inc(sa["logit_sb"], 1)
                dve.drain()
                for i in range(NT):
                    steps.done(v.max(top8[:, i, :], logit[:, i, 0:E]))
                steps.wait()
                steps.done(v.tensor_tensor(lsum[:], top8[:, :, 0], top8[:, :, 1], ALU.add))
                v.tensor_copy(pick[:, :, 0:2], top8[:, :, 0:2])
                steps.wait()
                v.scalar_tensor_tensor(out=lmid[:], in0=lsum[:].unsqueeze(2).broadcast_to((P, NT, E)), scalar=-0.5,
                                       in1=logit[:, :, 0:E], op0=ALU.mult, op1=ALU.add).then_inc(sa["lmid_sb"], 1)
                dve.drain()
                for i in range(NT):
                    steps.done(v.match_replace(marked[:, i, 0:E + 6], pick[:, i, :], logit[:, i, 0:E + 6], -BIG))
                steps.wait()
                steps.done(v.tensor_tensor(chosen[:], marked[:, :, 0:E], logit[:, :, 0:E], ALU.not_equal))

            def route_weights(b, steps):
                dve.wait_ge(sa["ltanh_sb"], b + 1)
                steps.done(v.tensor_scalar(wsig[:], ltanh[:], 0.5, 0.5, ALU.mult, ALU.add))
                steps.wait()
                steps.done(v.tensor_tensor(wfull[:], chosen[:], wsig[:], ALU.mult))
                steps.wait()
                steps.done(v.tensor_copy(wround[:], wfull[:]))
                steps.wait()
                v.tensor_copy(wpad[:, :, 0:E], wround[:].bitcast(F32))
                v.tensor_tensor(wpad[:, :, LO_ROW:KW], wfull[:], wround[:].bitcast(F32),
                                ALU.subtract).then_inc(sa["wpad_sb"], 1)

            def keep_weights(b):
                dve.wait_ge(sa["wT_pe"], b + 1)
                v.tensor_copy(wT[:, bass.ds(b * SEQ, SEQ)], ps_x1[0:KW, :]).then_inc(sa["wT_sb"], 1)

            dve.wait_ge(sa["q_sb"], 1)
            v.tensor_copy(q_h[:], q_all[:, 0:SEQ]).then_inc(sa["qh_sb"], 1)
            dve.wait_ge(sa["qh_sb"], 1)
            v.tensor_tensor(q_l[:], q_all[:, 0:SEQ], q_h[:].bitcast(F32), ALU.subtract).then_inc(sa["ql_sb"], 1)
            k_high(0)
            dve.wait_ge(ss["wvoh_sb"], 1)
            v.tensor_tensor(WvoT_l[:], bank[3][:, P:2 * P], WvoT_h[:].bitcast(F32), ALU.subtract).then_inc(ss["wvol_sb"], 1)
            row_max(0)
            k_high(1)
            weight_low(0, Wg_raw[:], Wg_h[:], Wg_l[:])
            value_low(0)
            value_low(1)
            weight_low(1, Wu_raw[:], Wu_h[:], Wu_l[:])
            for b in range(2, NB):
                k_high(b)
                value_low(b)

            def attention(b, steps, first=False):
                sum_inverse(b)
                probsT_low(b, 0)
                if not first:
                    norm_bias(b - 1)
                probsT_low(b, 1)
                probsT_low(b, 2)
                row_max(b + 1)
                if not first:
                    x1T_low(b - 1)
                    route_top2(b - 1, steps)
                    route_weights(b - 1, steps)
                residual(b, steps)
                if not first:
                    keep_weights(b - 1)

            attention(0, st, first=True)
            per = NT + (NT + 1 + NT + 1) + 3
            with dve.Fori(1, NB - 1) as b:
                steps = Steps(dve, dve_step, (b - 1) * per + st.n)
                attention(b, steps)
            assert steps.n == per, steps.n

            st.n += per * (NB - 2)
            sum_inverse(NB - 1)
            probsT_low(NB - 1, 0)
            norm_bias(NB - 2)
            probsT_low(NB - 1, 1)
            probsT_low(NB - 1, 2)

            def times_up(g, j):
                n = g * NCH + j
                dve.wait_ge(sf["silu_sb"], n + 1)
                dve.wait_ge(sf["up_pe"], n + 1)
                if j < NSH:
                    need(dve, sf["hTl_sb"], n - 1)
                    v.tensor_tensor(hid[j % 2], ps_up[j % 2][:], silu[j % 2], ALU.mult).then_inc(sf["su_sb"], 1)
                else:
                    v.tensor_tensor(su[j % 2], ps_up[j % 2][:], silu[j % 2], ALU.mult).then_inc(sf["su_sb"], 1)

            def times_weight(g, j):
                n = g * NCH + j
                if j < NSH:
                    return
                dve.wait_ge(sf["su_sb"], n + 1)
                dve.wait_ge(sf["w_pe"], g * NRT + j - NSH + 1)
                need(dve, sf["hTl_sb"], n - 1)
                v.tensor_tensor(hid[j % 2], ps_w[j % 2][:], su[j % 2], ALU.mult).then_inc(sf["hid_sb"], 1)

            def residual2(g):
                dve.wait_ge(sf["yT_pe"], g + 1)
                v.tensor_tensor(r2, ps_out[:].rearrange("p (i c) -> p i c", c=C),
                                x1_all[:, bass.ds(g * NT, NT), :], ALU.add).then_inc(sf["r2_sb"], 1)

            def row_stats2(g, steps):
                dve.wait_ge(sf["r2_sb"], g + 1)
                row_stats(steps, r2, stats2, mv2, veps2, sf["ln2var_sb"])

            def normalise2(g):
                dve.wait_ge(sf["ln2rstd_sb"], g + 1)
                need(dve, out_stored, 16 * g, PRIMED)
                for i in range(NT):
                    ins = v.tensor_scalar(o_tok[:, i, :], r2[:, i, :], mv2[:, i, 0:1], lrstd2[:, i:i + 1],
                                          ALU.subtract, ALU.mult)
                ins.then_inc(sf["o_sb"], 1)

            def group(g, steps, first=False):
                for j in range(NCH):
                    times_up(g, j)
                    times_weight(g, j)
                    if not first:
                        if j == 4:
                            residual2(g - 1)
                        if j == 6:
                            row_stats2(g - 1, steps)
                        if j == 10:
                            normalise2(g - 1)
                    else:
                        if j == 0:
                            x1T_low(NB - 2)
                        if j == 1:
                            residual(NB - 1, steps)
                        if j == 2:
                            route_top2(NB - 2, steps)
                            route_weights(NB - 2, steps)
                        if j == 3:
                            norm_bias(NB - 1)
                        if j == 4:
                            keep_weights(NB - 2)
                        if j == 6:
                            x1T_low(NB - 1)
                        if j == 8:
                            route_top2(NB - 1, steps)
                        if j == 9:
                            route_weights(NB - 1, steps)
                        if j == 11:
                            keep_weights(NB - 1)

            group(0, st, first=True)
            with dve.Fori(1, NB) as g:
                steps = Steps(dve, dve_step, (g - 1) * NT + st.n)
                group(g, steps)
            assert steps.n == NT
            st.n += NT * (NB - 1)
            residual2(NB - 1)
            row_stats2(NB - 1, st)
            normalise2(NB - 1)


_INS = ["L0_attn_x", "L0_attn_W_attn", "L0_attn_W_proj", "L0_attn_lora_attn_A", "L0_attn_lora_attn_B",
        "L0_attn_lora_proj_A", "L0_attn_lora_proj_B", "L0_attn_bn_gamma", "L0_attn_bn_beta", "L0_ffn_gate_w",
        "L0_ffn_exp_gate", "L0_ffn_exp_up", "L0_ffn_exp_down", "L0_ffn_sh_gate", "L0_ffn_sh_up", "L0_ffn_sh_down"]


def kernel(**inputs):
    import concourse.bacc as bacc
    from concourse.bass_utils import run_bass_kernel_spmd

    nc = bacc.Bacc("TRN2", target_bir_lowering=False, num_devices=1)
    arrays, args = {}, []
    for name in _INS:
        a = np.ascontiguousarray(inputs[name])
        arrays[f"{name}_dram"] = a
        args.append(nc.dram_tensor(f"{name}_dram", a.shape, mybir.dt.from_np(a.dtype), kind="ExternalInput").ap())
    x = inputs["L0_attn_x"]
    args.append(nc.dram_tensor("out_dram", x.shape, F32, kind="ExternalOutput").ap())
    block_kernel(nc, *args)
    r = run_bass_kernel_spmd(nc, [arrays], core_ids=[0])
    return r.results[0]["out_dram"]
```

```python
from contextlib import ExitStack

import numpy as np

import concourse.bass as bass
from concourse import mybir

ALU = mybir.AluOpType
ACT = mybir.ActivationFunctionType
AX = mybir.AxisListType
F32 = mybir.dt.float32
F32R = mybir.dt.float32r

P = 128
EPS = 1e-5
MASKED = -1.0e30
BIG = 3.0e38


def need(eng, sem, value, start=0):
    if isinstance(value, int) and value <= 0:
        return
    eng.wait_ge(sem, value + start)


class Steps:

    def __init__(self, eng, sem, base=0):
        self.eng, self.sem, self.base, self.n = eng, sem, base, 0

    def done(self, ins):
        self.n += 1
        ins.then_inc(self.sem, 1)

    def wait(self):
        self.eng.wait_ge(self.sem, self.base + self.n)


def block_kernel(nc, w_dram, x, W_attn, W_proj, attn_A, attn_B, proj_A, proj_B, bn_gamma, bn_beta,
                 gate_w, exp_gate, exp_up, exp_down, sh_gate, sh_up, sh_down, out):
    NB, SEQ, C = x.shape
    R = attn_A.shape[1]
    D3 = W_attn.shape[0]
    NJ = D3 // C
    E, _, F = exp_gate.shape
    S = sh_gate.shape[0]
    NT = SEQ // P
    NTOK = NB * SEQ
    SCALE = float(C) ** -0.5
    SHF = S * F
    NSH = -(-SHF // P)
    NCH = NSH + E * F // P
    NRT = NCH - NSH
    SH_TAIL = SHF - (NSH - 1) * P
    FT = NCH * P
    NWB = 4
    assert C == P and E * F % P == 0 and NT * P == SEQ and NCH % 2 == 0 and E == 8

    xv = x.rearrange("b (i p) c -> b p i c", p=P)
    ov = out.rearrange("b (i p) c -> b p i c", p=P)

    with ExitStack() as ctx:
        def sb(name, shape, dt=F32):
            return ctx.enter_context(nc.sbuf_tensor(name, shape, dt))

        def sem(name):
            return ctx.enter_context(nc.semaphore(name))

        bank = [ctx.enter_context(nc.psum_tensor(f"bank{i}", [P, 512], F32)) for i in range(8)]
        ps_proj = [bank[0], bank[2]]
        ps_score = bank[5:8]
        ps_pT = [bank[3], bank[4], bank[0]]
        ps_y, ps_x1 = bank[1], bank[2]
        ps_gate, ps_up = bank[5:7], [bank[7], bank[3]]
        ps_down, ps_out = bank[1], bank[2]

        proj_turns = [(0, 0), (0, 1)] + [(b, n) for b in range(1, NB) for n in range(NJ)]

        def proj_bank(b, n):
            return ps_y if (b, n) == (0, 2) else ps_proj[proj_turns.index((b, n)) % 2]

        def pT_bank(first, n):
            return ps_y if first and n == 2 else ps_pT[n]

        score_at = [(0, 0), (0, P), (1, 0), (2, 0)]
        prob_off = [i * (i + 1) // 2 * P for i in range(NT + 1)]
        pT_parts = [(0, 2), (2, 1), (3, 1)]

        x_tok = sb("x_tok", [P, NB * NT, C + 2])
        xT_h = sb("xT_h", [P, NTOK], F32R)
        xT_l = sb("xT_l", [P, NTOK], F32R)
        Wm = sb("Wm", [P, NJ, C])
        WmT = sb("WmT", [P, D3])
        WqkT_h = sb("WqkT_h", [P, 2 * C], F32R)
        WqkT_l = sb("WqkT_l", [P, 2 * C], F32R)
        loA = sb("loA", [P, R])
        loB = sb("loB", [R, D3])
        loAT = sb("loAT", [R, P])
        pA = sb("pA", [P, R])
        pB = sb("pB", [R, C])
        pAT = sb("pAT", [R, P])
        Wp = sb("Wp", [P, C])
        Wmp = sb("Wmp", [P, C])
        WmpT = sb("WmpT", [P, C])
        W2T = sb("W2T", [P, C])
        W2s = sb("W2s", [P, C])
        Wv = sb("Wv", [P, C])
        WvoT_h = sb("WvoT_h", [P, C], F32R)
        WvoT_l = sb("WvoT_l", [P, C], F32R)
        gram = sb("gram", [P, C + 2])
        wgw = sb("wgw", [P, D3])
        bn_rows = sb("bn_rows", [2 * NJ, C])
        bn_cols = sb("bn_cols", [P, 2 * NJ])
        mean = sb("mean", [P, NJ])
        msq = sb("msq", [P, NJ])
        var = sb("var", [P, NJ])
        rstd = sb("rstd", [P, NJ])
        bn_s = sb("bn_s", [P, NJ])
        bn_t = sb("bn_t", [P, NJ])
        mst = sb("mst", [P, NJ])
        qk_s = sb("qk_s", [P, 2])
        qk_t = sb("qk_t", [P, 2])
        tv_b = sb("tv_b", [P, P])
        bias_tok = sb("bias_tok", [P, C])
        x_res = sb("x_res", [P, NT, C])
        q_all = sb("q_all", [P, NTOK + SEQ])
        kf = sb("kf", [P, SEQ])
        q_h = sb("q_h", [P, SEQ], F32R)
        q_l = sb("q_l", [P, SEQ], F32R)
        k_h = sb("k_h", [P, NTOK], F32R)
        k_l = sb("k_l", [P, NTOK], F32R)
        v_h = sb("v_h", [P, NB * NT, C], F32R)
        v_l = sb("v_l", [P, NB * NT, C], F32R)
        negmax = sb("negmax", [P, NT])
        rowsum = sb("rowsum", [P, NT])
        rinv = sb("rinv", [P, NT])
        prob = sb("prob", [P, prob_off[NT]])
        pT_h = sb("pT_h", [P, prob_off[NT]], F32R)
        pT_l = sb("pT_l", [P, prob_off[NT]], F32R)
        res1 = sb("res1", [P, NT, C])
        stats = sb("stats", [P, NT, 6])
        mv = sb("mv", [P, NT, 2])
        veps = sb("veps", [P, NT])
        lrstd = sb("lrstd", [P, NT])
        negmean = sb("negmean", [P, NT])
        nmr = sb("nmr", [P, NT])
        x1cur = sb("x1cur", [P, NT, C])
        x1_all = x_tok[:, :, 0:C]
        x1T_h = sb("x1T_h", [P, SEQ], F32R)
        x1T_l = sb("x1T_l", [P, SEQ], F32R)
        x1Ta_h, x1Ta_l = xT_h, xT_l
        gw = sb("gw", [P, E])
        gw_h = sb("gw_h", [P, E], F32R)
        gw_l = sb("gw_l", [P, E], F32R)
        logit = sb("logit", [P, NB * NT, 2 * E])
        top8 = sb("top8", [P, NB * NT, 8])
        pick = sb("pick", [P, NB * NT, 8])
        marked = sb("marked", [P, NB * NT, 2 * E])
        chosen = sb("chosen", [P, NB * NT, E])
        lsum = sb("lsum", [P, NB * NT])
        lmid = sb("lmid", [P, NB * NT, E])
        ltanh = sb("ltanh", [P, NB * NT, E])
        wsig = sb("wsig", [P, NB * NT, E])
        wpad = sb("wpad", [P, NB * NT, P])
        wT = sb("wT", [E, 2, SEQ])
        wb = [sb(f"wb{n}", [P, SEQ]) for n in range(NWB)]
        Wg_raw = sb("Wg_raw", [P, FT])
        Wu_raw = sb("Wu_raw", [P, FT])
        Wd_raw = sb("Wd_raw", [P, NCH, C])
        Wg_h = sb("Wg_h", [P, FT], F32R)
        Wg_l = sb("Wg_l", [P, FT], F32R)
        Wu_h = sb("Wu_h", [P, FT], F32R)
        Wu_l = sb("Wu_l", [P, FT], F32R)
        Wd_h = sb("Wd_h", [P, NCH, C], F32R)
        Wd_l = sb("Wd_l", [P, NCH, C], F32R)
        silu = [Wg_raw[:, 0:SEQ], Wg_raw[:, SEQ:2 * SEQ]]
        su = [Wg_raw[:, 2 * SEQ:3 * SEQ], Wu_raw[:, 0:SEQ]]
        hid = [Wu_raw[:, SEQ:2 * SEQ], Wu_raw[:, 2 * SEQ:3 * SEQ]]
        wd_flat = Wd_raw[:].rearrange("p k c -> p (k c)")
        y_sb = wd_flat[:, 0:SEQ]
        r2 = wd_flat[:, SEQ:2 * SEQ].rearrange("p (i c) -> p i c", c=C)
        o_tok = wd_flat[:, 2 * SEQ:3 * SEQ].rearrange("p (i c) -> p i c", c=C)
        hT_h = [k_h[:, n * SEQ:(n + 1) * SEQ] for n in range(NB)]
        hT_l = [k_l[:, n * SEQ:(n + 1) * SEQ] for n in range(NB)]
        stats2 = sb("stats2", [P, NT, 6])
        mv2 = sb("mv2", [P, NT, 2])
        veps2 = sb("veps2", [P, NT])
        lrstd2 = sb("lrstd2", [P, NT])
        ident = sb("ident", [P, P])
        ident_r = sb("ident_r", [P, P], F32R)
        mask_f = sb("mask_f", [P, P])
        mask_r = sb("mask_r", [P, P], F32R)
        ones = sb("ones", [P, P])
        warm = sb("warm", [P, P])
        nhalf = sb("nhalf", [P, NT])

        x_in = [sem(f"x_in{b}") for b in range(NB)]
        wa_in, loraA_in, loraB_in = map(sem, ("wa_in", "loraA_in", "loraB_in"))
        wp_in, bn_in, gw_in = map(sem, ("wp_in", "bn_in", "gw_in"))
        wg_in, wu_in, wd_in = map(sem, ("wg_in", "wu_in", "wd_in"))
        x1_kept, x1T_kept, out_stored = map(sem, ("x1_kept", "x1T_kept", "out_stored"))
        pool_const = sem("pool_const")
        dve_const = sem("dve_const")
        warm_sb = sem("warm_sb")
        names = ("loraAT_pe loraAT_sb lora_pe wm_sb xT_pe xTh_sb xTl_sb wmT_pe wmT_sb wmpT_pe wmpT_sb gram_pe gram_sb "
                 "w2_pe w2_sb gw_pe wgw_sb means_pe moments_pe wv_sb bn_var bn_rstd bn_ready w2s_sb wvo_pe wvoh_sb wvol_sb bias_pe "
                 "bias_sb tvb_sb wqkh_sb wqkl_sb gwh_sb gwl_sb").split()
        ss = {n: sem(n) for n in names}
        dve_step = sem("dve_step")
        names = ("rinv_sb nmr_sb q_pe q_sb qh_sb ql_sb k_pe k_sb kh_sb kl_sb v_pe vh_sb vl_sb score_pe max_sb prob_sb pT_pe pTh_sb "
                 "pTl_sb y_pe xres_sb res_free lnvar_sb lnrstd_sb x1_sb x1T_pe x1Th_sb x1Tl_sb logit_pe logit_sb "
                 "lmid_sb ltanh_sb wpad_sb wT_pe wT_sb").split()
        sa = {n: sem(n) for n in names}
        names = ("wgh_sb wuh_sb wdh_sb wsplit_l gate_pe up_pe silu_sb su_sb hid_sb hTh_sb hTl_sb "
                 "down_pe y_sbd yT_pe r2_sb ln2var_sb ln2rstd_sb o_sb").split()
        sf = {n: sem(n) for n in names}

        names = "last_high last_low last_y last_yT last_r2 last_var last_rstd last_out".split()
        sl = {n: sem(n) for n in names}

        w_stored = [sem("w_stored0"), sem("w_stored1")]
        wb_in = [sem(f"wb_in{n}") for n in range(NWB)]

        LAG = 3
        HT_SLOT = [n for length in (4, 4, 3, 3) for n in range(length)]
        assert len(HT_SLOT) == NCH and NB >= 4

        ROUTED_AT = 10

        def ht_reuse(j):
            return next(d for d in range(1, NCH + 1) if HT_SLOT[(j - d) % NCH] == HT_SLOT[j])

        def chunk_experts(c):
            lo, hi = c * P, (c + 1) * P
            return [(e, max(lo, e * F) - lo, min(hi, (e + 1) * F) - lo) for e in range(lo // F, (hi - 1) // F + 1)]

        def wb_loads(c):
            return sum(len(chunk_experts(i)) for i in range(c % NWB, c + 1, NWB))

        wb_last = [max(range(n, NRT, NWB)) for n in range(NWB)]

        block = ctx.enter_context(nc.Block())

        CONST_ONES, CONST_PAD, CONST_IDENT, CONST_MASK, CONST_FILL = 1, 2, 4, 5, 6
        PRIMED = 1
        SUMS, SQUARES = 256, 160
        WARM_UP = 6

        def blk(i):
            return slice(i * P, (i + 1) * P)

        HALF = NT // 2
        half = [slice(h * HALF * P, (h + 1) * HALF * P) for h in range(2)]
        half_tiles = [slice(h * HALF, (h + 1) * HALF) for h in range(2)]
        last_out_bank = [ps_out, bank[4]]

        @block.sync
        def _(sp):
            for b in range(NB):
                sp.dma_start(x_tok[:, b * NT:(b + 1) * NT, 0:C], xv[b]).then_inc(x_in[b], 16)
            sp.dma_start(Wm[:].rearrange("c j k -> c (j k)"),
                         W_attn.rearrange("(c j) k -> c (j k)", j=NJ)).then_inc(wa_in, 16)
            sp.dma_start(Wp[:], W_proj).then_inc(wp_in, 16)
            sp.dma_start(bn_rows[0:NJ, :], bn_gamma.rearrange("(j d) -> j d", d=C)).then_inc(bn_in, 16)
            sp.dma_start(bn_rows[NJ:2 * NJ, :], bn_beta.rearrange("(j d) -> j d", d=C)).then_inc(bn_in, 16)
            sp.dma_start(gw[:], gate_w).then_inc(gw_in, 16)
            sp.wait_ge(pool_const, CONST_PAD)
            for raw, shared, routed, done in ((Wu_raw, sh_up, exp_up, wu_in), (Wg_raw, sh_gate, exp_gate, wg_in)):
                sp.dma_start(raw[:, 0:SHF].rearrange("c (s f) -> c s f", s=S),
                             shared.rearrange("s c f -> c s f")).then_inc(done, 16)
                sp.dma_start(raw[:, NSH * P:FT].rearrange("c (e f) -> c e f", e=E),
                             routed.rearrange("e c f -> c e f")).then_inc(done, 16)
            shd = sh_down.rearrange("s f c -> (s f) c")
            sp.dma_start(Wd_raw[:, 0:NSH - 1, :],
                         shd[0:(NSH - 1) * P].rearrange("(k p) c -> p k c", p=P)).then_inc(wd_in, 16)
            sp.dma_start(Wd_raw[0:SH_TAIL, NSH - 1, :], shd[(NSH - 1) * P:SHF]).then_inc(wd_in, 16)
            sp.dma_start(Wd_raw[:, NSH:NCH, :],
                         exp_down.rearrange("e f c -> (e f) c").rearrange("(k p) c -> p k c", p=P)).then_inc(wd_in, 16)

            def keep_x1(b):
                need(sp, x1_kept, 16 * b, PRIMED)
                sp.wait_ge(sa["x1_sb"], b + 1)
                sp.dma_start(x1_all[:, bass.ds(b * NT, NT), :], x1cur[:]).then_inc(x1_kept, 16)

            def keep_x1T(b):
                sp.wait_ge(sa["x1Tl_sb"], b + 1)
                sp.dma_start(x1Ta_h[:, bass.ds(b * SEQ, SEQ)].bitcast(F32), x1T_h[:].bitcast(F32)).then_inc(x1T_kept, 16)
                sp.dma_start(x1Ta_l[:, bass.ds(b * SEQ, SEQ)].bitcast(F32), x1T_l[:].bitcast(F32)).then_inc(x1T_kept, 16)

            def store_weights(b):
                sp.wait_ge(sa["wT_sb"], b + 1)
                sp.dma_start(w_dram[b], wT[:, b % 2, :]).then_inc(w_stored[b % 2], 16)

            def load_weights(g, c):
                if c == 0:
                    sp.wait_ge(w_stored[g % 2], 16 * (g // 2) + 16)
                used = g * NRT + c - NWB + 1 if c >= NWB else (g - 1) * NRT + wb_last[c] + 1
                need(sp, sf["hid_sb"], used)
                for e, lo, hi in chunk_experts(c):
                    sp.dma_start(wb[c % NWB][lo:hi, :],
                                 w_dram[g, e].partition_broadcast(hi - lo)).then_inc(wb_in[c % NWB], 16)

            def store(g):
                need(sp, out_stored, 16 * g, PRIMED)
                sp.wait_ge(sf["o_sb"], g + 1)
                sp.dma_start(ov[g], o_tok[:]).then_inc(out_stored, 16)

            for b in range(NB - 2):
                keep_x1(b)
                keep_x1T(b)
            store_weights(0)
            keep_x1(NB - 2)
            for c in range(NWB):
                load_weights(0, c)
            keep_x1T(NB - 2)
            for c in range(NWB, NRT):
                load_weights(0, c)
                if c == 5:
                    keep_x1(NB - 1)
                if c == 7:
                    keep_x1T(NB - 1)
            store_weights(1)
            for g in range(1, NB):
                for c in range(NRT):
                    load_weights(g, c)
                    if g == 1 and 2 <= c < NB:
                        store_weights(c)
                store(g - 1)
            need(sp, out_stored, 16 * (NB - 1), PRIMED)
            for h, tiles in enumerate(half_tiles):
                sp.wait_ge(sl["last_out"], h + 1)
                sp.dma_start(ov[NB - 1][:, tiles, :], o_tok[:, tiles, :]).then_inc(out_stored, 16)
            for done in w_stored:
                sp.wait_ge(done, 16 * NB // 2)
            sp.wait_ge(out_stored, 16 * (NB + 1) + PRIMED)

        @block.gpsimd
        def _(pool):
            made = [0]

            def const(ins):
                made[0] += 1
                ins.then_inc(pool_const, 1)
                pool.wait_ge(pool_const, made[0])

            g = nc.gpsimd
            const(g.memset(x_tok[:, :, C:C + 2], 1.0))
            g.memset(Wg_raw[:, SHF:NSH * P], 0.0)
            g.memset(Wu_raw[:, SHF:NSH * P], 0.0)
            const(g.memset(Wd_raw[:, NSH - 1, :], 0.0))
            g.memset(ones[:], 1.0).then_inc(x1_kept, PRIMED)
            g.memset(nhalf[:], -0.5).then_inc(out_stored, PRIMED)
            const(g.memset(mask_f[:], 0.0))
            const(g.affine_select(out=ident[:], in_=ones[:], compare_op=ALU.is_equal, fill=0.0, base=0,
                                  pattern=[[-1, P]], channel_multiplier=1))
            const(g.affine_select(out=mask_f[:], in_=mask_f[:], compare_op=ALU.is_ge, fill=MASKED, base=0,
                                  pattern=[[-1, P]], channel_multiplier=1))
            g.memset(logit[:], BIG)
            g.memset(pick[:], BIG).then_inc(x1T_kept, PRIMED)
            const(g.memset(wpad[:], 0.0))
            assert made[0] == CONST_FILL
            pool.wait_ge(ss["bn_var"], 1)
            nc.gpsimd.tensor_tensor(out=rstd[:], in0=var[:], in1=nhalf[:, 0:NJ], op=ALU.pow).then_inc(ss["bn_rstd"], 1)

            def split_q(b):
                pool.wait_ge(sa["qh_sb"], b + 1)
                nc.gpsimd.tensor_tensor(out=q_l[:], in0=q_all[:, bass.ds(b * SEQ, SEQ)], in1=q_h[:].bitcast(F32),
                                        op=ALU.subtract).then_inc(sa["ql_sb"], 1)

            def split_k(b):
                cols = slice(b * SEQ, (b + 1) * SEQ)
                pool.wait_ge(sa["kh_sb"], b + 1)
                nc.gpsimd.tensor_tensor(out=k_l[:, cols], in0=kf[:], in1=k_h[:, cols].bitcast(F32),
                                        op=ALU.subtract).then_inc(sa["kl_sb"], 1)

            def residual_base(b):
                need(pool, sa["res_free"], b)
                nc.gpsimd.tensor_tensor(out=x_res[:], in0=x_tok[:, bass.ds(b * NT, NT), 0:C],
                                        in1=bias_tok[:].unsqueeze(1).broadcast_to((P, NT, C)),
                                        op=ALU.add).then_inc(sa["xres_sb"], 1)

            def ln_rstd(b):
                pool.wait_ge(sa["lnvar_sb"], b + 1)
                nc.gpsimd.tensor_tensor(out=lrstd[:], in0=veps[:], in1=nhalf[:], op=ALU.pow).then_inc(sa["lnrstd_sb"], 1)
                pool.wait_ge(sa["lnrstd_sb"], b + 1)
                nc.gpsimd.tensor_tensor(out=nmr[:], in0=negmean[:], in1=lrstd[:], op=ALU.mult).then_inc(sa["nmr_sb"], 1)

            def split_weight(hi_ready, raw, hi, lo):
                pool.wait_ge(sf[hi_ready], 1)
                nc.gpsimd.tensor_tensor(out=lo[:], in0=raw[:], in1=hi[:].bitcast(F32),
                                        op=ALU.subtract).then_inc(sf["wsplit_l"], 1)

            def split_hidden(g, j):
                n = g * NCH + j
                pool.wait_ge(sf["hTh_sb"], n + 1)
                nc.gpsimd.tensor_tensor(out=hT_l[HT_SLOT[j]], in0=hid[j % 2], in1=hT_h[HT_SLOT[j]].bitcast(F32),
                                        op=ALU.subtract).then_inc(sf["hTl_sb"], 1)

            def ln2_rstd(g):
                pool.wait_ge(sf["ln2var_sb"], g + 1)
                nc.gpsimd.tensor_tensor(out=lrstd2[:], in0=veps2[:], in1=nhalf[:], op=ALU.pow).then_inc(sf["ln2rstd_sb"], 1)

            nc.gpsimd.memset(q_all[:, NTOK:NTOK + SEQ], 0.0).then_inc(sa["logit_sb"], PRIMED)
            split_q(0)
            pool.wait_ge(ss["bias_sb"], 1)
            residual_base(0)
            split_k(1)
            split_q(1)
            split_weight("wuh_sb", Wu_raw, Wu_h, Wu_l)
            split_q(2)
            split_weight("wdh_sb", Wd_raw, Wd_h, Wd_l)
            ln_rstd(0)
            split_weight("wgh_sb", Wg_raw, Wg_h, Wg_l)
            with pool.Fori(1, NB - 1) as b:
                residual_base(b)
                split_q(b + 2)
                ln_rstd(b)
            residual_base(NB - 1)
            split_hidden(0, 0)
            ln_rstd(NB - 1)

            for j in range(1, NCH - 1):
                split_hidden(0, j)
            with pool.Fori(1, NB) as g:
                split_hidden(g - 1, NCH - 1)
                for j in range(NCH - 1):
                    split_hidden(g, j)
                    if j == 7:
                        ln2_rstd(g - 1)
            for h, tiles in enumerate(half_tiles):
                pool.wait_ge(sl["last_var"], h + 1)
                nc.gpsimd.tensor_tensor(out=lrstd2[:, tiles], in0=veps2[:, tiles], in1=nhalf[:, tiles],
                                        op=ALU.pow).then_inc(sl["last_rstd"], 1)

        @block.tensor
        def _(pe):
            def mm3(dst, lh, ll, rh, rl, start=True, stop=True):
                nc.tensor.matmul(dst, lh, rh, start=start, stop=False)
                nc.tensor.matmul(dst, lh, rl, start=False, stop=False)
                return nc.tensor.matmul(dst, ll, rh, start=False, stop=stop)

            def gram_of(b):
                pe.wait_ge(x_in[b], 16)
                for t in range(b * NT, (b + 1) * NT):
                    last = nc.tensor.matmul(bank[3][:, 0:C + 1], x_tok[:, t, 0:C], x_tok[:, t, 0:C + 1],
                                            start=(t == 0), stop=(t == NB * NT - 1))
                if b == NB - 1:
                    last.then_inc(ss["gram_pe"], 1)

            def transpose_x(b):
                for i in range(NT):
                    last = nc.tensor.transpose(bank[4 + b][:, blk(i)], x_tok[:, b * NT + i, 0:C], ident[:])
                last.then_inc(ss["xT_pe"], 1)

            pe.wait_ge(warm_sb, 1)
            for _ in range(WARM_UP):
                nc.tensor.matmul(bank[7][:, 0:P], warm[:], warm[:], start=True, stop=True)
            pe.wait_ge(pool_const, CONST_ONES)
            gram_of(0)
            pe.wait_ge(pool_const, CONST_IDENT)
            pe.wait_ge(loraA_in, 32)
            nc.tensor.transpose(bank[0][0:R, 0:P], loA[:], ident[:])
            nc.tensor.transpose(bank[0][0:R, P:2 * P], pA[:], ident[:]).then_inc(ss["loraAT_pe"], 1)
            gram_of(1)
            pe.wait_ge(ss["loraAT_sb"], 1)
            pe.wait_ge(loraB_in, 32)
            nc.tensor.matmul(bank[1][:, 0:D3], loAT[:], loB[:], start=True, stop=True).then_inc(ss["lora_pe"], 1)
            nc.tensor.matmul(bank[2][:, 0:C], pAT[:], pB[:], start=True, stop=True).then_inc(ss["lora_pe"], 1)
            gram_of(2)
            pe.wait_ge(ss["wm_sb"], 2)
            for j in range(NJ):
                last = nc.tensor.transpose(bank[0][:, blk(j)], Wm[:, j, :], ident[:])
            last.then_inc(ss["wmT_pe"], 1)
            nc.tensor.transpose(bank[2][:, 0:C], Wmp[:], ident[:]).then_inc(ss["wmpT_pe"], 1)
            gram_of(3)
            transpose_x(0)
            pe.wait_ge(ss["wmpT_sb"], 1)
            nc.tensor.matmul(bank[2][:, P:2 * P], Wp[:], WmpT[:], start=True, stop=True).then_inc(ss["w2_pe"], 1)
            pe.wait_ge(ss["gram_sb"], 1)
            pe.wait_ge(ss["wmT_sb"], 1)
            nc.tensor.matmul(bank[1][:, 0:D3], gram[:, 0:C], WmT[:], start=True, stop=True).then_inc(ss["gw_pe"], 1)
            for j in range(NJ):
                last = nc.tensor.matmul(bank[3][:, SUMS + j:SUMS + j + 1], WmT[:, blk(j)], gram[:, C:C + 1],
                                        start=True, stop=True)
            last.then_inc(ss["means_pe"], 1)
            nc.tensor.transpose(bank[0][:, 0:C], WmT[:, 2 * C:3 * C], ident[:])
            pe.wait_ge(bn_in, 32)
            nc.tensor.transpose(bank[0][:, P:P + 2 * NJ], bn_rows[:], ident[0:2 * NJ, 0:2 * NJ])
            pe.wait_ge(ss["wgw_sb"], 1)
            for j in range(NJ):
                last = nc.tensor.matmul(bank[0][:, SQUARES + j:SQUARES + j + 1], wgw[:, blk(j)], ones[:, 0:1],
                                        start=True, stop=True)
            last.then_inc(ss["moments_pe"], 1)
            transpose_x(1)
            transpose_x(2)
            transpose_x(3)

            def project_q(b):
                cols = slice(b * SEQ, (b + 1) * SEQ)
                mm3(proj_bank(b, 0)[:], WqkT_h[:, blk(0)], WqkT_l[:, blk(0)], xT_h[:, cols],
                    xT_l[:, cols]).then_inc(sa["q_pe"], 1)

            def project_k(b):
                cols = slice(b * SEQ, (b + 1) * SEQ)
                mm3(proj_bank(b, 1)[:], WqkT_h[:, blk(1)], WqkT_l[:, blk(1)], xT_h[:, cols],
                    xT_l[:, cols]).then_inc(sa["k_pe"], 1)

            def project_v(b):
                for i in range(NT):
                    t = b * NT + i
                    last = mm3(proj_bank(b, 2)[:, blk(i)], xT_h[:, blk(t)], xT_l[:, blk(t)], WvoT_h[:], WvoT_l[:])
                last.then_inc(sa["v_pe"], 1)

            def scores(b):
                pe.wait_ge(sa["ql_sb"], b + 1)
                pe.wait_ge(sa["kl_sb"], b + 1)
                need(pe, sa["prob_sb"], NT * b)
                for i in range(NT):
                    w = (i + 1) * P
                    n, at = score_at[i]
                    dst = ps_score[n]
                    mm3(dst[:, at:at + w], q_h[:, blk(i)], q_l[:, blk(i)], k_h[:, bass.ds(b * SEQ, w)],
                        k_l[:, bass.ds(b * SEQ, w)], stop=False)
                    nc.tensor.matmul(dst[:, at + i * P:at + w], ident_r[:], mask_r[:], start=False,
                                     stop=True).then_inc(sa["score_pe"], 1)

            def transpose_probs(b, parts=(0, 1, 2), first=False):
                for n in parts:
                    i0, tiles = pT_parts[n]
                    pe.wait_ge(sa["prob_sb"], NT * b + i0 + tiles)
                    o = prob_off[i0]
                    for c in range((prob_off[i0 + tiles] - o) // P):
                        last = nc.tensor.transpose(pT_bank(first, n)[:, blk(c)], prob[:, o + c * P:o + (c + 1) * P],
                                                   ident[:])
                    last.then_inc(sa["pT_pe"], 1)

            def attend(b, parts=(0, 1, 2), first=False):
                if first:
                    pe.wait_ge(sa["pTl_sb"], 3)
                elif 0 in parts:
                    pe.wait_ge(sa["res_free"], b)
                for n in parts:
                    i0, tiles = pT_parts[n]
                    pe.wait_ge(sa["pTl_sb"], 3 * b + n + 1)
                    for i in range(i0, i0 + tiles):
                        for j in range(i + 1):
                            at = prob_off[i] + j * P
                            last = mm3(ps_y[:, blk(i)], pT_h[:, at:at + P], pT_l[:, at:at + P],
                                       v_h[:, bass.ds(b * NT + j, 1), :].rearrange("p a c -> p (a c)"),
                                       v_l[:, bass.ds(b * NT + j, 1), :].rearrange("p a c -> p (a c)"),
                                       start=(j == 0), stop=(j == i))
                if 2 in parts:
                    last.then_inc(sa["y_pe"], 1)

            def transpose_x1(b):
                pe.wait_ge(sa["x1_sb"], b + 1)
                for i in range(NT):
                    last = nc.tensor.transpose(ps_x1[:, blk(i)], x1cur[:, i, :], ident[:])
                last.then_inc(sa["x1T_pe"], 1)

            def logits(b):
                pe.wait_ge(sa["x1Tl_sb"], b + 1)
                for i in range(NT):
                    last = mm3(ps_x1[:, i * E:(i + 1) * E], x1T_h[:, blk(i)], x1T_l[:, blk(i)], gw_h[:], gw_l[:])
                last.then_inc(sa["logit_pe"], 1)

            def transpose_w(b):
                pe.wait_ge(sa["wpad_sb"], 1 if b == 0 else 2)
                for i in range(NT):
                    last = nc.tensor.transpose(ps_x1[:, blk(i)], wpad[:, b * NT + i, :], ident[:])
                last.then_inc(sa["wT_pe"], 1)

            pe.wait_ge(ss["xTl_sb"], 1)
            pe.wait_ge(ss["wqkl_sb"], 1)
            pe.wait_ge(ss["wv_sb"], 1)
            project_q(0)
            pe.wait_ge(ss["w2_sb"], 1)
            project_k(0)
            pe.wait_ge(ss["w2s_sb"], 1)
            nc.tensor.matmul(bank[3][:, P:2 * P], Wv[:], W2s[:], start=True, stop=True).then_inc(ss["wvo_pe"], 1)
            pe.wait_ge(ss["tvb_sb"], 1)
            nc.tensor.matmul(bank[4][:, 0:C], tv_b[:], W2T[:], start=True, stop=True).then_inc(ss["bias_pe"], 1)

            pe.wait_ge(ss["xTl_sb"], 2)
            pe.wait_ge(sa["q_sb"], 1)
            project_q(1)
            pe.wait_ge(sa["k_sb"], 1)
            project_k(1)
            pe.wait_ge(ss["wvol_sb"], 1)
            project_v(0)
            pe.wait_ge(dve_const, 2)
            pe.wait_ge(ss["xTl_sb"], NB)
            scores(0)
            pe.wait_ge(sa["q_sb"], 2)
            project_v(1)
            transpose_probs(0, (0, 1), first=True)
            pe.wait_ge(sa["k_sb"], 2)
            project_q(2)
            pe.wait_ge(sa["vl_sb"], 1)
            transpose_probs(0, (2,), first=True)
            scores(1)
            pe.wait_ge(sa["vl_sb"], 2)
            project_k(2)
            attend(0, first=True)
            pe.wait_ge(sa["q_sb"], 3)
            project_v(2)
            pe.wait_ge(sa["k_sb"], 3)
            project_q(3)
            transpose_probs(1, (0, 1))
            pe.wait_ge(sa["vl_sb"], 3)
            project_k(3)
            pe.wait_ge(sa["q_sb"], NB)
            project_v(3)
            pe.wait_ge(sa["res_free"], 1)
            transpose_probs(1, (2,), first=True)
            pe.wait_ge(ss["gwl_sb"], 1)

            with pe.Fori(1, NB - 1) as b:
                scores(b + 1)
                pe.wait_ge(sa["pTl_sb"], 6)
                attend(b, (0,))
                pe.wait_ge(sa["k_sb"], NB)
                need(pe, sa["logit_sb"], b - 1, PRIMED)
                transpose_x1(b - 1)
                attend(b, (1, 2))
                logits(b - 1)
                transpose_probs(b + 1, (0, 1))
                pe.wait_ge(sa["vl_sb"], NB)
                transpose_probs(b + 1, (2,))

            def up_chunk(g, j):
                n = g * NCH + j
                if j == 0:
                    pe.wait_ge(x1_kept, 16 * g + 16 + PRIMED)
                    pe.wait_ge(x1T_kept, 32 * g + 32 + PRIMED)
                xh, xl = x1Ta_h[:, bass.ds(g * SEQ, SEQ)], x1Ta_l[:, bass.ds(g * SEQ, SEQ)]
                need(pe, sf["silu_sb"], n - 1)
                mm3(ps_gate[j % 2][:], Wg_h[:, blk(j)], Wg_l[:, blk(j)], xh, xl).then_inc(sf["gate_pe"], 1)
                need(pe, sf["su_sb"], n - 1)
                mm3(ps_up[j % 2][:], Wu_h[:, blk(j)], Wu_l[:, blk(j)], xh, xl).then_inc(sf["up_pe"], 1)

            def down_chunk(g, j):
                n = g * NCH + j
                if j == 0:
                    need(pe, sf["y_sbd"], g)
                pe.wait_ge(sf["hTl_sb"], n + 1)
                mm3(ps_down[:], Wd_h[:, j, :], Wd_l[:, j, :], hT_h[HT_SLOT[j]], hT_l[HT_SLOT[j]],
                    start=(j == 0), stop=(j == NCH - 1)).then_inc(sf["down_pe"], 1)

            def transpose_y(g):
                pe.wait_ge(sf["y_sbd"], g + 1)
                for i in range(NT):
                    last = nc.tensor.transpose(ps_out[:, blk(i)], y_sb[:, blk(i)], ident[:])
                last.then_inc(sf["yT_pe"], 1)

            def group(g, first=False):
                for j in range(NCH):
                    up_chunk(g, j)
                    if first and j == LAG:
                        pe.wait_ge(sa["res_free"], NB)
                    if first and j == 4:
                        logits(NB - 2)
                    if first and j == 6:
                        pe.wait_ge(sa["logit_sb"], NB - 1 + PRIMED)
                        transpose_x1(NB - 1)
                    if first and 0 <= j - ROUTED_AT < NB - 1:
                        if j == ROUTED_AT:
                            pe.wait_ge(sa["logit_sb"], NB + PRIMED)
                        else:
                            pe.wait_ge(sa["wT_sb"], j - ROUTED_AT + 1)
                        transpose_w(j - ROUTED_AT + 1)
                    if j >= LAG:
                        down_chunk(g, j - LAG)
                    elif not first:
                        down_chunk(g - 1, NCH - LAG + j)
                    if j == 3 and not first:
                        transpose_y(g - 1)
                    if first:
                        if j == 0:
                            attend(NB - 1, (0, 1))
                        if j == 1:
                            attend(NB - 1, (2,))
                            pe.wait_ge(sa["logit_sb"], NB - 2 + PRIMED)
                            transpose_w(0)
                        if j == 2:
                            pe.wait_ge(sa["wT_sb"], 1)
                            transpose_x1(NB - 2)
                        if j == 7:
                            logits(NB - 1)

            pe.wait_ge(sf["wsplit_l"], 3)
            group(0, first=True)
            pe.wait_ge(sa["wT_sb"], NB)
            with pe.Fori(1, NB) as g:
                group(g)
            for j in range(NCH - LAG, NCH - 1):
                down_chunk(NB - 1, j)
            slot = HT_SLOT[NCH - 1]
            for h, cols in enumerate(half):
                pe.wait_ge(sl["last_low"], h + 1)
                last = mm3(ps_down[:, cols], Wd_h[:, NCH - 1, :], Wd_l[:, NCH - 1, :],
                           hT_h[slot][:, cols], hT_l[slot][:, cols], start=False, stop=(h == 1))
            last.then_inc(sf["down_pe"], 1)
            for h in range(2):
                pe.wait_ge(sl["last_y"], h + 1)
                for i in range(HALF):
                    last = nc.tensor.transpose(last_out_bank[h][:, blk(i)], y_sb[:, blk(h * HALF + i)], ident[:])
                last.then_inc(sl["last_yT"], 1)

        @block.scalar
        def _(act):
            act.dma_start(loA[:], attn_A).then_inc(loraA_in, 16)
            act.dma_start(pA[:], proj_A).then_inc(loraA_in, 16)
            act.dma_start(loB[:], attn_B).then_inc(loraB_in, 16)
            act.dma_start(pB[:], proj_B).then_inc(loraB_in, 16)
            act.preload_act_table(ACT.Exp)

            act.wait_ge(ss["loraAT_pe"], 1)
            nc.scalar.activation(loAT[:], bank[0][0:R, 0:P], ACT.Copy)
            nc.scalar.activation(pAT[:], bank[0][0:R, P:2 * P], ACT.Copy).then_inc(ss["loraAT_sb"], 1)

            def xT_high(b):
                act.wait_ge(ss["xT_pe"], b + 1)
                nc.scalar.activation(xT_h[:, b * SEQ:(b + 1) * SEQ], bank[4 + b][:], ACT.Copy).then_inc(ss["xTh_sb"], 1)

            act.wait_ge(ss["wmT_pe"], 1)
            nc.scalar.activation(WmT[:].rearrange("p (c j) -> p j c", j=NJ),
                                 bank[0][:, 0:D3].rearrange("p (j c) -> p j c", j=NJ), ACT.Copy).then_inc(ss["wmT_sb"], 1)
            act.wait_ge(ss["wmpT_pe"], 1)
            nc.scalar.activation(WmpT[:], bank[2][:, 0:C], ACT.Copy).then_inc(ss["wmpT_sb"], 1)
            act.wait_ge(ss["gram_pe"], 1)
            nc.scalar.activation(gram[:, 0:C + 1], bank[3][:, 0:C + 1], ACT.Copy).then_inc(ss["gram_sb"], 1)
            xT_high(0)
            act.wait_ge(ss["w2_pe"], 1)
            nc.scalar.activation(W2T[:], bank[2][:, P:2 * P], ACT.Copy).then_inc(ss["w2_sb"], 1)
            act.wait_ge(ss["wmT_sb"], 1)
            nc.scalar.activation(WqkT_h[:], WmT[:, 0:2 * C], ACT.Copy).then_inc(ss["wqkh_sb"], 1)

            def affine_q(b):
                act.wait_ge(sa["q_pe"], b + 1)
                nc.scalar.activation(q_all[:, b * SEQ:(b + 1) * SEQ], proj_bank(b, 0)[:], ACT.Identity, bias=qk_t[:, 0:1],
                                     scale=qk_s[:, 0:1]).then_inc(sa["q_sb"], 1)

            def affine_k(b):
                act.wait_ge(sa["k_pe"], b + 1)
                need(act, sa["kl_sb"], b)
                nc.scalar.activation(kf[:], proj_bank(b, 1)[:], ACT.Identity, bias=qk_t[:, 1:2],
                                     scale=qk_s[:, 1:2]).then_inc(sa["k_sb"], 1)

            def value_high(b):
                act.wait_ge(sa["v_pe"], b + 1)
                nc.scalar.activation(v_h[:, b * NT:(b + 1) * NT, :].rearrange("p i c -> p (i c)"),
                                     proj_bank(b, 2)[:], ACT.Copy).then_inc(sa["vh_sb"], 1)

            def probs(b, tiles):
                if 0 in tiles:
                    need(act, sa["rinv_sb"], b)
                for i in tiles:
                    act.wait_ge(sa["max_sb"], NT * b + max(2, i + 1))
                    n, at = score_at[i]
                    nc.scalar.activation(prob[:, prob_off[i]:prob_off[i + 1]], ps_score[n][:, at:at + (i + 1) * P],
                                         ACT.Exp, bias=negmax[:, i:i + 1],
                                         accum_out=rowsum[:, i:i + 1]).then_inc(sa["prob_sb"], 1)

            def q_high(b):
                nc.scalar.activation(q_h[:], q_all[:, bass.ds(b * SEQ, SEQ)], ACT.Copy).then_inc(sa["qh_sb"], 1)

            def probsT_high(b, n, first=False):
                act.wait_ge(sa["pT_pe"], 3 * b + n + 1)
                i0, tiles = pT_parts[n]
                lo, hi = prob_off[i0], prob_off[i0 + tiles]
                nc.scalar.activation(pT_h[:, lo:hi], pT_bank(first, n)[:, 0:hi - lo], ACT.Copy).then_inc(sa["pTh_sb"], 1)

            def normalise(b, tiles=range(NT)):
                need(act, x1_kept, 16 * b, PRIMED)
                act.wait_ge(sa["nmr_sb"], b + 1)
                for i in tiles:
                    ins = nc.scalar.activation(x1cur[:, i, :], res1[:, i, :], ACT.Identity, bias=nmr[:, i:i + 1],
                                               scale=lrstd[:, i:i + 1])
                if NT - 1 in tiles:
                    ins.then_inc(sa["x1_sb"], 1)

            def x1T_high(b):
                need(act, x1T_kept, 32 * b, PRIMED)
                act.wait_ge(sa["x1T_pe"], b + 1)
                nc.scalar.activation(x1T_h[:], ps_x1[:], ACT.Copy).then_inc(sa["x1Th_sb"], 1)

            def router_tanh(n, tiles):
                act.wait_ge(sa["lmid_sb"], n + 1)
                nc.scalar.activation(ltanh[:, tiles, :], lmid[:, tiles, :], ACT.Tanh).then_inc(sa["ltanh_sb"], 1)

            act.wait_ge(wu_in, 32)
            nc.scalar.activation(Wu_h[:], Wu_raw[:], ACT.Copy).then_inc(sf["wuh_sb"], 1)
            xT_high(1)
            xT_high(2)
            xT_high(3)
            act.wait_ge(ss["bn_ready"], 1)
            affine_q(0)
            act.wait_ge(ss["wvo_pe"], 1)
            nc.scalar.activation(WvoT_h[:], bank[3][:, P:2 * P], ACT.Copy).then_inc(ss["wvoh_sb"], 1)
            affine_k(0)
            act.wait_ge(ss["bias_pe"], 1)
            nc.scalar.activation(bias_tok[:], bank[4][:, 0:C], ACT.Copy).then_inc(ss["bias_sb"], 1)
            affine_q(1)
            affine_k(1)
            value_high(0)
            probs(0, range(NT))
            value_high(1)
            probsT_high(0, 0, first=True)
            probsT_high(0, 1, first=True)
            affine_q(2)
            probsT_high(0, 2, first=True)
            act.wait_ge(wd_in, 48)
            nc.scalar.activation(Wd_h[:], Wd_raw[:], ACT.Copy).then_inc(sf["wdh_sb"], 1)
            probs(1, (0, 1))
            affine_k(2)
            probs(1, (2, 3))
            value_high(2)
            affine_q(3)
            probsT_high(1, 0)
            probsT_high(1, 1)
            affine_k(3)
            value_high(3)
            probsT_high(1, 2, first=True)
            act.wait_ge(sa["q_sb"], NB)
            normalise(0)
            with act.Fori(1, NB - 1) as b:
                probs(b + 1, (0, 1))
                x1T_high(b - 1)
                probs(b + 1, (2, 3))
                q_high(b + 2)
                for n in range(3):
                    probsT_high(b + 1, n)
                normalise(b)
            act.preload_act_table(ACT.Silu)
            router_tanh(0, slice(0, NT))

            def gate_silu(g, j):
                n = g * NCH + j
                act.wait_ge(sf["gate_pe"], n + 1)
                need(act, sf["su_sb"], n - 1)
                nc.scalar.activation(silu[j % 2], ps_gate[j % 2][:], ACT.Silu).then_inc(sf["silu_sb"], 1)

            def hidden_high(g, j):
                n = g * NCH + j
                if j < NSH:
                    act.wait_ge(sf["su_sb"], n + 1)
                else:
                    act.wait_ge(sf["hid_sb"], g * NRT + j - NSH + 1)
                need(act, sf["down_pe"], n - ht_reuse(j) + 1)
                nc.scalar.activation(hT_h[HT_SLOT[j]], hid[j % 2], ACT.Copy).then_inc(sf["hTh_sb"], 1)

            def down_out(g):
                act.wait_ge(sf["down_pe"], (g + 1) * NCH)
                nc.scalar.activation(y_sb, ps_down[:], ACT.Copy).then_inc(sf["y_sbd"], 1)

            def group(g, first=False):
                for j in range(NCH):
                    gate_silu(g, j)
                    if j >= 1:
                        hidden_high(g, j - 1)
                    elif not first:
                        hidden_high(g - 1, NCH - 1)
                    if j == 2 and not first:
                        down_out(g - 1)
                    if first:
                        if j == 2:
                            x1T_high(NB - 2)
                        if j == 4:
                            normalise(NB - 1, (0, 1))
                        if j == 5:
                            normalise(NB - 1, (2, 3))
                        if j == 6:
                            x1T_high(NB - 1)
                        if j == 8:
                            router_tanh(2, slice(NT, NB * NT))

            act.wait_ge(sf["wsplit_l"], 3)
            group(0, first=True)
            with act.Fori(1, NB) as g:
                group(g)
            act.wait_ge(sf["hid_sb"], NB * NRT)
            act.wait_ge(sf["down_pe"], NB * NCH - ht_reuse(NCH - 1))
            for cols in half:
                nc.scalar.activation(hT_h[HT_SLOT[NCH - 1]][:, cols], hid[(NCH - 1) % 2][:, cols],
                                     ACT.Copy).then_inc(sl["last_high"], 1)
            act.wait_ge(sf["down_pe"], NB * NCH)
            for cols in half:
                nc.scalar.activation(y_sb[:, cols], ps_down[:, cols], ACT.Copy).then_inc(sl["last_y"], 1)

        @block.vector
        def _(dve):
            v = nc.vector
            st = Steps(dve, dve_step)
            v.memset(warm[:], 1.0).then_inc(warm_sb, 1)
            dve.wait_ge(pool_const, CONST_MASK)
            v.tensor_copy(ident_r[:], ident[:]).then_inc(dve_const, 1)
            v.tensor_copy(mask_r[:], mask_f[:]).then_inc(dve_const, 1)
            dve.wait_ge(ss["lora_pe"], 1)
            dve.wait_ge(wa_in, 16)
            wm_flat = Wm[:].rearrange("c j k -> c (j k)")
            v.tensor_tensor(wm_flat, bank[1][:, 0:D3], wm_flat, ALU.add).then_inc(ss["wm_sb"], 1)
            dve.wait_ge(ss["lora_pe"], 2)
            dve.wait_ge(wp_in, 16)
            v.tensor_tensor(Wmp[:], bank[2][:, 0:C], Wp[:], ALU.add).then_inc(ss["wm_sb"], 1)

            def xT_low(b):
                dve.wait_ge(ss["xTh_sb"], b + 1)
                cols = slice(b * SEQ, (b + 1) * SEQ)
                v.tensor_tensor(xT_l[:, cols], bank[4 + b][:], xT_h[:, cols].bitcast(F32),
                                ALU.subtract).then_inc(ss["xTl_sb"], 1)

            dve.wait_ge(ss["gw_pe"], 1)
            v.tensor_tensor(wgw[:], bank[1][:, 0:D3], WmT[:], ALU.mult).then_inc(ss["wgw_sb"], 1)
            dve.wait_ge(ss["means_pe"], 1)
            st.done(v.tensor_scalar(mean[:], bank[3][:, SUMS:SUMS + NJ], 1.0 / NTOK, None, ALU.mult))
            dve.wait_ge(ss["wqkh_sb"], 1)
            v.tensor_tensor(WqkT_l[:], WmT[:, 0:2 * C], WqkT_h[:].bitcast(F32), ALU.subtract).then_inc(ss["wqkl_sb"], 1)
            st.wait()
            st.done(v.tensor_tensor(msq[:], mean[:], mean[:], ALU.mult))
            xT_low(0)
            dve.wait_ge(ss["moments_pe"], 1)
            st.wait()
            st.done(v.scalar_tensor_tensor(out=var[:], in0=bank[0][:, SQUARES:SQUARES + NJ], scalar=1.0 / NTOK, in1=msq[:],
                                           op0=ALU.mult, op1=ALU.subtract))
            st.done(v.tensor_copy(bn_cols[:], bank[0][:, P:P + 2 * NJ]))
            st.wait()
            v.tensor_scalar(var[:], var[:], 0.0, EPS, ALU.max, ALU.add).then_inc(ss["bn_var"], 1)
            v.tensor_copy(Wv[:], bank[0][:, 0:C]).then_inc(ss["wv_sb"], 1)
            xT_low(1)
            dve.wait_ge(ss["bn_rstd"], 1)
            st.done(v.tensor_tensor(bn_s[:], rstd[:], bn_cols[:, 0:NJ], ALU.mult))
            st.wait()
            st.done(v.tensor_tensor(mst[:], mean[:], bn_s[:], ALU.mult))
            v.tensor_scalar(qk_s[:, 0:1], bn_s[:, 0:1], SCALE, None, ALU.mult)
            v.tensor_copy(qk_s[:, 1:2], bn_s[:, 1:2])
            st.wait()
            st.done(v.tensor_tensor(bn_t[:], bn_cols[:, NJ:2 * NJ], mst[:], ALU.subtract))
            st.wait()
            v.tensor_scalar(qk_t[:, 0:1], bn_t[:, 0:1], SCALE, None, ALU.mult)
            v.tensor_copy(qk_t[:, 1:2], bn_t[:, 1:2]).then_inc(ss["bn_ready"], 1)
            dve.wait_ge(ss["w2_sb"], 1)
            v.tensor_scalar(W2s[:], W2T[:], bn_s[:, 2:3], None, ALU.mult).then_inc(ss["w2s_sb"], 1)
            v.tensor_scalar(tv_b[:], ones[:], bn_t[:, 2:3], None, ALU.mult).then_inc(ss["tvb_sb"], 1)
            xT_low(2)

            def k_high(b):
                dve.wait_ge(sa["k_sb"], b + 1)
                v.tensor_copy(k_h[:, b * SEQ:(b + 1) * SEQ], kf[:]).then_inc(sa["kh_sb"], 1)

            def value_low(b):
                dve.wait_ge(sa["vh_sb"], b + 1)
                tiles = slice(b * NT, (b + 1) * NT)
                v.tensor_tensor(v_l[:, tiles, :].rearrange("p i c -> p (i c)"), proj_bank(b, 2)[:],
                                v_h[:, tiles, :].rearrange("p i c -> p (i c)").bitcast(F32),
                                ALU.subtract).then_inc(sa["vl_sb"], 1)

            def row_max(b):
                for i in range(NT):
                    dve.wait_ge(sa["score_pe"], NT * b + max(2, i + 1))
                    n, at = score_at[i]
                    v.tensor_reduce(negmax[:, i:i + 1], ps_score[n][:, at:at + (i + 1) * P], AX.X, ALU.max,
                                    negate=True).then_inc(sa["max_sb"], 1)

            def probsT_low(b, n, first=False):
                dve.wait_ge(sa["pTh_sb"], 3 * b + n + 1)
                i0, tiles = pT_parts[n]
                lo, hi = prob_off[i0], prob_off[i0 + tiles]
                v.tensor_tensor(pT_l[:, lo:hi], pT_bank(first, n)[:, 0:hi - lo], pT_h[:, lo:hi].bitcast(F32),
                                ALU.subtract).then_inc(sa["pTl_sb"], 1)

            def row_stats(steps, src, st6, mean_var, var_eps, var_ready, neg_mean=None, tiles=slice(0, NT)):
                for i in range(tiles.start, tiles.stop):
                    v.bn_stats(st6[:, i, :], src[:, i, :])
                dve.drain()
                for i in range(tiles.start, tiles.stop):
                    steps.done(v.bn_aggr(mean_var[:, i, :], st6[:, i, :]))
                steps.wait()
                if neg_mean is not None:
                    v.tensor_scalar(neg_mean[:], mean_var[:, :, 0], -1.0, None, ALU.mult)
                v.tensor_scalar(var_eps[:, tiles], mean_var[:, tiles, 1], EPS, None, ALU.add).then_inc(var_ready, 1)

            def sum_inverse(b):
                dve.wait_ge(sa["prob_sb"], NT * b + NT)
                v.reciprocal(rinv[:], rowsum[:]).then_inc(sa["rinv_sb"], 1)

            def residual(b):
                dve.wait_ge(sa["rinv_sb"], b + 1)
                need(dve, sa["x1_sb"], b)
                dve.wait_ge(sa["xres_sb"], b + 1)
                dve.wait_ge(sa["y_pe"], b + 1)
                for i in range(NT):
                    ins = v.scalar_tensor_tensor(out=res1[:, i, :], in0=ps_y[:, blk(i)], scalar=rinv[:, i:i + 1],
                                                 in1=x_res[:, i, :], op0=ALU.mult, op1=ALU.add)
                ins.then_inc(sa["res_free"], 1)

            def ln_stats(b, steps):
                dve.wait_ge(sa["res_free"], b + 1)
                row_stats(steps, res1, stats, mv, veps, sa["lnvar_sb"], negmean)

            def x1T_low(b):
                dve.wait_ge(sa["x1Th_sb"], b + 1)
                v.tensor_tensor(x1T_l[:], ps_x1[:], x1T_h[:].bitcast(F32), ALU.subtract).then_inc(sa["x1Tl_sb"], 1)

            def keep_logits(b):
                dve.wait_ge(sa["logit_pe"], b + 1)
                v.tensor_copy(logit[:, bass.ds(b * NT, NT), 0:E],
                              ps_x1[:, 0:NT * E].rearrange("p (i e) -> p i e", e=E)).then_inc(sa["logit_sb"], 1)

            def route_max(tiles):
                dve.wait_ge(sa["logit_sb"], tiles.stop // NT + PRIMED)
                for i in range(tiles.start, tiles.stop):
                    st.done(v.max(top8[:, i, :], logit[:, i, 0:E]))
                st.wait()
                st.done(v.tensor_tensor(lsum[:, tiles], top8[:, tiles, 0], top8[:, tiles, 1], ALU.add))
                st.done(v.tensor_copy(pick[:, tiles, 0:2], top8[:, tiles, 0:2]))
                st.wait()
                sums = lsum[:, tiles].unsqueeze(2).broadcast_to((P, tiles.stop - tiles.start, E))
                v.scalar_tensor_tensor(out=lmid[:, tiles, :], in0=sums, scalar=-0.5, in1=logit[:, tiles, 0:E],
                                       op0=ALU.mult, op1=ALU.add).then_inc(sa["lmid_sb"], 1)

            def route_choose(tiles):
                for i in range(tiles.start, tiles.stop):
                    st.done(v.match_replace(marked[:, i, 0:E + 6], pick[:, i, :], logit[:, i, 0:E + 6], -BIG))
                st.wait()
                st.done(v.tensor_tensor(chosen[:, tiles, :], marked[:, tiles, 0:E], logit[:, tiles, 0:E],
                                        ALU.not_equal))

            def route_weights(n, tiles):
                dve.wait_ge(sa["ltanh_sb"], n + 1)
                st.done(v.tensor_scalar(wsig[:, tiles, :], ltanh[:, tiles, :], 0.5, 0.5, ALU.mult, ALU.add))
                st.wait()
                v.tensor_tensor(wpad[:, tiles, 0:E], chosen[:, tiles, :], wsig[:, tiles, :],
                                ALU.mult).then_inc(sa["wpad_sb"], 1)

            def keep_weights(b):
                dve.wait_ge(sa["wT_pe"], b + 1)
                need(dve, w_stored[b % 2], 16 * (b // 2))
                v.tensor_copy(wT[:, b % 2, :], ps_x1[0:E, :]).then_inc(sa["wT_sb"], 1)

            def q_high(b):
                dve.wait_ge(sa["q_sb"], b + 1)
                v.tensor_copy(q_h[:], q_all[:, b * SEQ:(b + 1) * SEQ]).then_inc(sa["qh_sb"], 1)

            def k_low(b):
                cols = slice(b * SEQ, (b + 1) * SEQ)
                dve.wait_ge(sa["kh_sb"], b + 1)
                v.tensor_tensor(k_l[:, cols], kf[:], k_h[:, cols].bitcast(F32), ALU.subtract).then_inc(sa["kl_sb"], 1)

            dve.wait_ge(ss["wvoh_sb"], 1)
            v.tensor_tensor(WvoT_l[:], bank[3][:, P:2 * P], WvoT_h[:].bitcast(F32), ALU.subtract).then_inc(ss["wvol_sb"], 1)
            q_high(0)
            k_high(0)
            k_low(0)
            xT_low(3)
            k_high(1)
            row_max(0)
            q_high(1)
            value_low(0)
            value_low(1)
            sum_inverse(0)
            probsT_low(0, 0, first=True)
            probsT_low(0, 1, first=True)
            probsT_low(0, 2, first=True)
            row_max(1)
            q_high(2)
            k_high(2)
            k_low(2)
            dve.wait_ge(wg_in, 32)
            v.tensor_copy(Wg_h[:], Wg_raw[:]).then_inc(sf["wgh_sb"], 1)
            dve.wait_ge(gw_in, 16)
            v.tensor_copy(gw_h[:], gw[:]).then_inc(ss["gwh_sb"], 1)
            residual(0)
            value_low(2)
            ln_stats(0, st)
            dve.wait_ge(ss["gwh_sb"], 1)
            v.tensor_tensor(gw_l[:], gw[:], gw_h[:].bitcast(F32), ALU.subtract).then_inc(ss["gwl_sb"], 1)
            sum_inverse(1)
            probsT_low(1, 0)
            probsT_low(1, 1)
            value_low(3)
            probsT_low(1, 2, first=True)
            k_high(3)
            k_low(3)
            per = NT
            with dve.Fori(1, NB - 1) as b:
                steps = Steps(dve, dve_step, (b - 1) * per + st.n)
                row_max(b + 1)
                x1T_low(b - 1)
                residual(b)
                ln_stats(b, steps)
                sum_inverse(b + 1)
                for n in range(3):
                    probsT_low(b + 1, n)
                keep_logits(b - 1)
            assert steps.n == per, steps.n

            st.n += per * (NB - 2)
            tiles_0, tiles_rest = slice(0, NT), slice(NT, NB * NT)
            tiles_mid, tiles_last = slice(NT, (NB - 1) * NT), slice((NB - 1) * NT, NB * NT)
            route_max(tiles_0)
            route_choose(tiles_0)
            route_weights(0, tiles_0)

            def times_up(g, j):
                n = g * NCH + j
                dve.wait_ge(sf["silu_sb"], n + 1)
                dve.wait_ge(sf["up_pe"], n + 1)
                if j < NSH:
                    need(dve, sf["hTl_sb"], n - 1)
                    v.tensor_tensor(hid[j % 2], ps_up[j % 2][:], silu[j % 2], ALU.mult).then_inc(sf["su_sb"], 1)
                else:
                    v.tensor_tensor(su[j % 2], ps_up[j % 2][:], silu[j % 2], ALU.mult).then_inc(sf["su_sb"], 1)

            def times_weight(g, j):
                n = g * NCH + j
                if j < NSH:
                    return
                dve.wait_ge(sf["su_sb"], n + 1)
                c = j - NSH
                dve.wait_ge(wb_in[c % NWB], 16 * (g * wb_loads(wb_last[c % NWB]) + wb_loads(c)))
                need(dve, sf["hTl_sb"], n - 1)
                v.tensor_tensor(hid[j % 2], wb[c % NWB][:], su[j % 2], ALU.mult).then_inc(sf["hid_sb"], 1)

            def residual2(g):
                dve.wait_ge(sf["yT_pe"], g + 1)
                v.tensor_tensor(r2, ps_out[:].rearrange("p (i c) -> p i c", c=C),
                                x1_all[:, bass.ds(g * NT, NT), :], ALU.add).then_inc(sf["r2_sb"], 1)

            def row_stats2(g, steps):
                dve.wait_ge(sf["r2_sb"], g + 1)
                row_stats(steps, r2, stats2, mv2, veps2, sf["ln2var_sb"])

            def normalise2(g):
                dve.wait_ge(sf["ln2rstd_sb"], g + 1)
                need(dve, out_stored, 16 * g, PRIMED)
                for i in range(NT):
                    ins = v.tensor_scalar(o_tok[:, i, :], r2[:, i, :], mv2[:, i, 0:1], lrstd2[:, i:i + 1],
                                          ALU.subtract, ALU.mult)
                ins.then_inc(sf["o_sb"], 1)

            def group(g, steps, first=False):
                for j in range(NCH):
                    times_up(g, j)
                    times_weight(g, j)
                    if not first:
                        if j == 4:
                            residual2(g - 1)
                        if j == 6:
                            row_stats2(g - 1, steps)
                        if j == 10:
                            normalise2(g - 1)
                    else:
                        if j == 1:
                            keep_weights(0)
                            residual(NB - 1)
                            ln_stats(NB - 1, steps)
                        if j == 2:
                            x1T_low(NB - 2)
                        if j == 4:
                            keep_logits(NB - 2)
                        if j == 5:
                            route_max(tiles_mid)
                        if j == 6:
                            x1T_low(NB - 1)
                            route_choose(tiles_mid)
                        if j == 7:
                            keep_logits(NB - 1)
                            route_max(tiles_last)
                        if j == 8:
                            route_choose(tiles_last)
                            route_weights(1, tiles_rest)
                        if 0 <= j - ROUTED_AT < NB - 1:
                            keep_weights(j - ROUTED_AT + 1)

            group(0, st, first=True)
            with dve.Fori(1, NB) as g:
                steps = Steps(dve, dve_step, (g - 1) * NT + st.n)
                group(g, steps)
            assert steps.n == NT
            st.n += NT * (NB - 1)
            slot = HT_SLOT[NCH - 1]
            for h, cols in enumerate(half):
                dve.wait_ge(sl["last_high"], h + 1)
                v.tensor_tensor(hT_l[slot][:, cols], hid[(NCH - 1) % 2][:, cols], hT_h[slot][:, cols].bitcast(F32),
                                ALU.subtract).then_inc(sl["last_low"], 1)
            for h, tiles in enumerate(half_tiles):
                dve.wait_ge(sl["last_yT"], h + 1)
                v.tensor_tensor(r2[:, tiles, :], last_out_bank[h][:, 0:HALF * C].rearrange("p (i c) -> p i c", c=C),
                                x1_all[:, (NB - 1) * NT + tiles.start:(NB - 1) * NT + tiles.stop, :],
                                ALU.add).then_inc(sl["last_r2"], 1)
                dve.wait_ge(sl["last_r2"], h + 1)
                row_stats(st, r2, stats2, mv2, veps2, sl["last_var"], tiles=tiles)
            need(dve, out_stored, 16 * (NB - 1), PRIMED)
            for h, tiles in enumerate(half_tiles):
                dve.wait_ge(sl["last_rstd"], h + 1)
                for i in range(tiles.start, tiles.stop):
                    ins = v.tensor_scalar(o_tok[:, i, :], r2[:, i, :], mv2[:, i, 0:1], lrstd2[:, i:i + 1],
                                          ALU.subtract, ALU.mult)
                ins.then_inc(sl["last_out"], 1)


_INS = ["L0_attn_x", "L0_attn_W_attn", "L0_attn_W_proj", "L0_attn_lora_attn_A", "L0_attn_lora_attn_B",
        "L0_attn_lora_proj_A", "L0_attn_lora_proj_B", "L0_attn_bn_gamma", "L0_attn_bn_beta", "L0_ffn_gate_w",
        "L0_ffn_exp_gate", "L0_ffn_exp_up", "L0_ffn_exp_down", "L0_ffn_sh_gate", "L0_ffn_sh_up", "L0_ffn_sh_down"]


def kernel(**inputs):
    import concourse.bacc as bacc
    from concourse.bass_utils import run_bass_kernel_spmd

    nc = bacc.Bacc("TRN2", target_bir_lowering=False, num_devices=1)
    arrays, args = {}, []
    for name in _INS:
        a = np.ascontiguousarray(inputs[name])
        arrays[f"{name}_dram"] = a
        args.append(nc.dram_tensor(f"{name}_dram", a.shape, mybir.dt.from_np(a.dtype), kind="ExternalInput").ap())
    x = inputs["L0_attn_x"]
    args.append(nc.dram_tensor("out_dram", x.shape, F32, kind="ExternalOutput").ap())
    E, SEQ = inputs["L0_ffn_gate_w"].shape[1], x.shape[1]
    w_dram = nc.dram_tensor("w_scratch", (x.shape[0], E, SEQ), F32, kind="Internal").ap()
    block_kernel(nc, w_dram, *args)
    r = run_bass_kernel_spmd(nc, [arrays], core_ids=[0])
    return r.results[0]["out_dram"]
```
